# Optimizing a Trainium2 kernel written in Bass

```python
import numpy as np
import jax
import jax.numpy as jnp

def _softmax(x, axis=-1):
    return jax.nn.softmax(x, axis=axis)

def _gelu(x):
    return jax.nn.gelu(x, approximate=True)

def _silu(x):
    return jax.nn.silu(x)

def _sigmoid(x):
    return jax.nn.sigmoid(x)

def _layernorm(x, axis=-1, eps=1e-05):
    m = jnp.mean(x, axis=axis, keepdims=True)
    v = jnp.var(x, axis=axis, keepdims=True)
    return (x - m) / jnp.sqrt(v + eps)

def _scatter_add(tgt, idx, src, axis=0):
    return tgt.at[idx].add(src)

def _segment_sum(src, seg, n):
    return jax.ops.segment_sum(src, seg, n)
kernel_name = 'mk_gps_d2_gnn_r8_6b84e8'

def setup_inputs(seed: int=0):
    np.random.seed(seed)
    _w = jnp.asarray

    def _rec_inputs():
        import jax
        import jax.numpy as jnp
        _gk = jax.random.key(seed)
        x = -0.000364 + 1 * jax.random.normal(jax.random.fold_in(_gk, 1), (1250, 768), jnp.float32)
        src = jax.random.randint(jax.random.fold_in(_gk, 2), (20000,), 0, 1250, jnp.int32)
        dst = jnp.minimum((1250 * jax.random.uniform(jax.random.fold_in(_gk, 3), (20000,)) ** 2.0).astype(jnp.int32), 9999)
        _o = jnp.argsort(dst, stable=True)
        src = src[_o]
        dst = dst[_o]
        return (x, src, dst)
    x, src, dst = _rec_inputs()

    def _L0_gnn_setup():
        import jax, jax.numpy as jnp
        import numpy as np
        N = 2500
        DEG = 16
        E = N * DEG
        H = 12
        DIN = 64
        DOUT = 64
        NEG_SLOPE = 0.2
        key = jax.random.key(seed)
        k_h, k_src, k_w, k_al, k_ar, k_wr = jax.random.split(key, 6)
        std = 1.414 * np.sqrt(2.0 / (DIN + DOUT))
        h = jax.random.normal(k_h, (N, H * DIN), dtype=jnp.float32)
        src = jax.random.randint(k_src, (E,), 0, N, dtype=jnp.int64)
        dst = jnp.repeat(jnp.arange(N, dtype=jnp.int64), DEG)
        W = jax.random.normal(k_w, (DOUT, DIN), dtype=jnp.float32) * std
        attn_l = jax.random.normal(k_al, (1, H, DOUT), dtype=jnp.float32) * std
        attn_r = jax.random.normal(k_ar, (1, H, DOUT), dtype=jnp.float32) * std
        W_res = jax.random.normal(k_wr, (DOUT, DIN), dtype=jnp.float32) * std
        return {'h': h, 'src': src, 'dst': dst, 'W': W, 'attn_l': attn_l, 'attn_r': attn_r, 'W_res': W_res}
    _L0_gnn_all = _L0_gnn_setup()
    _L0_gnn_in = {k: v for k, v in _L0_gnn_all.items() if k in ('W', 'attn_l', 'attn_r', 'W_res')}
    del _L0_gnn_all

    def _L0_mix_setup():
        import jax, jax.numpy as jnp
        import numpy as np
        NUM_HEADS = 12

        def _reference_tuple_inner(x, w_qkv, w_proj, b_proj):
            B, N, C = x.shape
            H = NUM_HEADS
            D = C // H
            qkv = (x @ w_qkv).reshape(B, N, 3, H, D)
            q = jnp.transpose(qkv[:, :, 0], (0, 2, 1, 3))
            k = jnp.transpose(qkv[:, :, 1], (0, 2, 1, 3))
            v = jnp.transpose(qkv[:, :, 2], (0, 2, 1, 3))
            q = jax.nn.elu(q) + 1.0
            k = jax.nn.elu(k) + 1.0
            attn = jnp.einsum('bhnd,bhmd->bhnm', q, k)
            attn = attn / jnp.sum(attn, axis=-1, keepdims=True)
            out = jnp.einsum('bhnm,bhmd->bhnd', attn, v)
            out = jnp.transpose(out, (0, 2, 1, 3)).reshape(B, N, C)
            out = out @ w_proj + b_proj
            return (out, attn)
        key = jax.random.key(seed)
        k1, k2, k3 = jax.random.split(key, 3)
        B, N, C = (2, 256, 768)
        x = jax.random.normal(k1, (B, N, C), dtype=jnp.float32)
        w_qkv = jax.random.normal(k2, (C, 3 * C), dtype=jnp.float32) * 0.02
        w_proj = jax.random.normal(k3, (C, C), dtype=jnp.float32) * 0.02
        b_proj = jnp.zeros((C,), dtype=jnp.float32)
        return {'x': x, 'w_qkv': w_qkv, 'w_proj': w_proj, 'b_proj': b_proj}
    _L0_mix_all = _L0_mix_setup()
    _L0_mix_in = {k: v for k, v in _L0_mix_all.items() if k in ('w_qkv', 'w_proj', 'b_proj')}
    del _L0_mix_all

    def _L0_ffn_setup():
        import jax, jax.numpy as jnp
        import numpy as np
        B, S, H = (4, 1024, 768)
        E, K = (8, 2)
        key = jax.random.key(seed)
        ks = jax.random.split(key, 5)
        scale = 1.0 / np.sqrt(H)
        x = jax.random.normal(ks[0], (B, S, H), dtype=jnp.float32)
        router_w = jax.random.uniform(ks[1], (E, H), jnp.float32, -scale, scale)
        router_b = jax.random.uniform(ks[2], (E,), jnp.float32, -scale, scale)
        expert_w = jax.random.uniform(ks[3], (E, H, H), jnp.float32, -scale, scale)
        expert_b = jax.random.uniform(ks[4], (E, H), jnp.float32, -scale, scale)
        return {'x': x, 'router_w': router_w, 'router_b': router_b, 'expert_w': expert_w, 'expert_b': expert_b}
    _L0_ffn_all = _L0_ffn_setup()
    _L0_ffn_in = {k: v for k, v in _L0_ffn_all.items() if k in ('router_w', 'router_b', 'expert_w', 'expert_b')}
    del _L0_ffn_all

    def _L1_gnn_setup():
        import jax, jax.numpy as jnp
        import numpy as np
        N_NODES = 1250
        D = 768
        N_EDGES = 20000

        def gcn_conv(x, W, b, src, dst, n_nodes):
            h = x @ W
            deg = jax.ops.segment_sum(jnp.ones_like(dst, dtype=h.dtype), dst, num_segments=n_nodes)
            dinv = jnp.where(deg > 0, jax.lax.rsqrt(deg), 0.0)
            norm = dinv[src] * dinv[dst]
            msgs = h[src] * norm[:, None]
            out = jax.ops.segment_sum(msgs, dst, num_segments=n_nodes)
            return out + b

        def add_self_loops(edge_index, n_nodes):
            loop = jnp.arange(n_nodes, dtype=edge_index.dtype)
            src = jnp.concatenate([edge_index[0], loop])
            dst = jnp.concatenate([edge_index[1], loop])
            return (src, dst)
        key = jax.random.key(seed)
        k1, k2, k3, k4 = jax.random.split(key, 4)
        x = jax.random.normal(k1, (N_NODES, D), dtype=jnp.float32)
        edge_index = jax.random.randint(k2, (2, N_EDGES), 0, N_NODES, dtype=jnp.int32)
        glorot = float(np.sqrt(6.0 / (D + D)))
        W1 = jax.random.uniform(k3, (D, D), jnp.float32, -glorot, glorot)
        W2 = jax.random.uniform(k4, (D, D), jnp.float32, -glorot, glorot)
        b1 = jnp.zeros((D,), jnp.float32)
        b2 = jnp.zeros((D,), jnp.float32)
        return {'x': x, 'W1': W1, 'b1': b1, 'W2': W2, 'b2': b2, 'edge_index': edge_index}
    _L1_gnn_all = _L1_gnn_setup()
    _L1_gnn_in = {k: v for k, v in _L1_gnn_all.items() if k in ('W1', 'b1', 'W2', 'b2')}
    del _L1_gnn_all

    def _L1_mix_setup():
        import jax, jax.numpy as jnp
        import numpy as np
        NUM_HEADS = 12

        def _l2_norm(t):
            return t / jnp.linalg.norm(t, axis=-2, keepdims=True)

        def _reference_tuple_inner(x, w_qkv, w_proj, b_proj):
            B, N, C = x.shape
            H = NUM_HEADS
            D = C // H
            qkv = (x @ w_qkv).reshape(B, N, 3, H, D).transpose(2, 0, 3, 1, 4)
            q, k, v = (qkv[0], qkv[1], qkv[2])
            q = _l2_norm(q)
            kT = _l2_norm(k).transpose(0, 1, 3, 2)
            sum_k = kT.sum(axis=-1)
            D_inv = 1.0 / (N + jnp.einsum('bhnd,bhd->bhd', q, sum_k))
            attn_matrix = jnp.einsum('bhnd,bhdn->bhdn', q, kT) * D_inv[..., None]
            matrix = jnp.einsum('bhnd,bhdn->bdhn', v, kT)
            y = jnp.einsum('bdhn,bhdn->bhnd', matrix, attn_matrix)
            y = y.transpose(0, 2, 1, 3).reshape(B, N, C)
            out = y @ w_proj + b_proj
            return (out, attn_matrix)
        key = jax.random.key(seed)
        k1, k2, k3 = jax.random.split(key, 3)
        B, N, C = (64, 1024, 768)
        x = jax.random.normal(k1, (B, N, C), dtype=jnp.float32)
        w_qkv = jax.random.normal(k2, (C, 3 * C), dtype=jnp.float32) * 0.02
        w_proj = jax.random.normal(k3, (C, C), dtype=jnp.float32) * 0.02
        b_proj = jnp.zeros((C,), dtype=jnp.float32)
        return {'x': x, 'w_qkv': w_qkv, 'w_proj': w_proj, 'b_proj': b_proj}
    _L1_mix_all = _L1_mix_setup()
    _L1_mix_in = {k: v for k, v in _L1_mix_all.items() if k in ('w_qkv', 'w_proj', 'b_proj')}
    del _L1_mix_all

    def _L1_ffn_setup():
        import jax, jax.numpy as jnp
        import numpy as np
        B, T, D, H, E = (4, 256, 768, 384, 8)
        key = jax.random.key(seed)
        ks = jax.random.split(key, 7)
        s_d = 1.0 / np.sqrt(D)
        s_h = 1.0 / np.sqrt(H)
        return {'x': jax.random.normal(ks[0], (B, T, D), dtype=jnp.float32), 'Wg': jax.random.normal(ks[1], (E, D), dtype=jnp.float32) * s_d, 'bg': jax.random.normal(ks[2], (E,), dtype=jnp.float32) * 0.01, 'W1': jax.random.normal(ks[3], (E, D, H), dtype=jnp.float32) * s_d, 'b1': jax.random.normal(ks[4], (E, H), dtype=jnp.float32) * s_d, 'W2': jax.random.normal(ks[5], (E, H, D), dtype=jnp.float32) * s_h, 'b2': jax.random.normal(ks[6], (E, D), dtype=jnp.float32) * s_h}
    _L1_ffn_all = _L1_ffn_setup()
    _L1_ffn_in = {k: v for k, v in _L1_ffn_all.items() if k in ('Wg', 'bg', 'W1', 'b1', 'W2', 'b2')}
    del _L1_ffn_all
    return {'x': x, 'src': src, 'dst': dst, 'L0_gnn_W': _L0_gnn_in['W'], 'L0_gnn_attn_l': _L0_gnn_in['attn_l'], 'L0_gnn_attn_r': _L0_gnn_in['attn_r'], 'L0_gnn_W_res': _L0_gnn_in['W_res'], 'L0_mix_w_qkv': _L0_mix_in['w_qkv'], 'L0_mix_w_proj': _L0_mix_in['w_proj'], 'L0_mix_b_proj': _L0_mix_in['b_proj'], 'L0_ffn_router_w': _L0_ffn_in['router_w'], 'L0_ffn_router_b': _L0_ffn_in['router_b'], 'L0_ffn_expert_w': _L0_ffn_in['expert_w'], 'L0_ffn_expert_b': _L0_ffn_in['expert_b'], 'L1_gnn_W1': _L1_gnn_in['W1'], 'L1_gnn_b1': _L1_gnn_in['b1'], 'L1_gnn_W2': _L1_gnn_in['W2'], 'L1_gnn_b2': _L1_gnn_in['b2'], 'L1_mix_w_qkv': _L1_mix_in['w_qkv'], 'L1_mix_w_proj': _L1_mix_in['w_proj'], 'L1_mix_b_proj': _L1_mix_in['b_proj'], 'L1_ffn_Wg': _L1_ffn_in['Wg'], 'L1_ffn_bg': _L1_ffn_in['bg'], 'L1_ffn_W1': _L1_ffn_in['W1'], 'L1_ffn_b1': _L1_ffn_in['b1'], 'L1_ffn_W2': _L1_ffn_in['W2'], 'L1_ffn_b2': _L1_ffn_in['b2']}

def reference(x, src, dst, L0_gnn_W, L0_gnn_attn_l, L0_gnn_attn_r, L0_gnn_W_res, L0_mix_w_qkv, L0_mix_w_proj, L0_mix_b_proj, L0_ffn_router_w, L0_ffn_router_b, L0_ffn_expert_w, L0_ffn_expert_b, L1_gnn_W1, L1_gnn_b1, L1_gnn_W2, L1_gnn_b2, L1_mix_w_qkv, L1_mix_w_proj, L1_mix_b_proj, L1_ffn_Wg, L1_ffn_bg, L1_ffn_W1, L1_ffn_b1, L1_ffn_W2, L1_ffn_b2):
    import jax
    import jax.numpy as jnp

    def _L0_gnn_ref(h, src, dst, W, attn_l, attn_r, W_res):
        import jax, jax.numpy as jnp
        import numpy as np
        N = 2500
        DEG = 16
        E = N * DEG
        H = 12
        DIN = 64
        DOUT = 64
        NEG_SLOPE = 0.2
        n = h.shape[0]
        hv = h.reshape(n, H, DIN)
        ft = jnp.einsum('nhd,od->nho', hv, W)
        a1 = jnp.sum(ft * attn_l, axis=-1)
        a2 = jnp.sum(ft * attn_r, axis=-1)
        e = jax.nn.leaky_relu(a1[src] + a2[dst], negative_slope=NEG_SLOPE)
        m = jax.ops.segment_max(e, dst, num_segments=n)
        m = jnp.where(jnp.isfinite(m), m, 0.0)
        w = jnp.exp(e - m[dst])
        denom = jax.ops.segment_sum(w, dst, num_segments=n)
        alpha = w / jnp.maximum(denom[dst], 1e-16)
        msg = alpha[:, :, None] * ft[src]
        agg = jax.ops.segment_sum(msg, dst, num_segments=n)
        res = jnp.einsum('nhd,od->nho', hv, W_res)
        out = jax.nn.relu((agg + res).reshape(n, H * DOUT))
        return out

    def _L0_mix_ref(x, w_qkv, w_proj, b_proj):
        import jax, jax.numpy as jnp
        import numpy as np
        NUM_HEADS = 12

        def _reference_tuple_inner(x, w_qkv, w_proj, b_proj):
            B, N, C = x.shape
            H = NUM_HEADS
            D = C // H
            qkv = (x @ w_qkv).reshape(B, N, 3, H, D)
            q = jnp.transpose(qkv[:, :, 0], (0, 2, 1, 3))
            k = jnp.transpose(qkv[:, :, 1], (0, 2, 1, 3))
            v = jnp.transpose(qkv[:, :, 2], (0, 2, 1, 3))
            q = jax.nn.elu(q) + 1.0
            k = jax.nn.elu(k) + 1.0
            attn = jnp.einsum('bhnd,bhmd->bhnm', q, k)
            attn = attn / jnp.sum(attn, axis=-1, keepdims=True)
            out = jnp.einsum('bhnm,bhmd->bhnd', attn, v)
            out = jnp.transpose(out, (0, 2, 1, 3)).reshape(B, N, C)
            out = out @ w_proj + b_proj
            return (out, attn)
        return _reference_tuple_inner(x, w_qkv, w_proj, b_proj)[0]

    def _L0_ffn_ref(x, router_w, router_b, expert_w, expert_b):
        import jax, jax.numpy as jnp
        import numpy as np
        B, S, H = (4, 1024, 768)
        E, K = (8, 2)
        scores = jnp.einsum('bsh,eh->bse', x, router_w) + router_b
        probs = jax.nn.softmax(scores, axis=-1)
        top_probs, expert_ids = jax.lax.top_k(probs, K)
        y = jnp.einsum('bsh,edh->bsed', x, expert_w) + expert_b
        out_k = jnp.take_along_axis(y, expert_ids[..., None], axis=2)
        w = top_probs / (jnp.sum(top_probs, axis=-1, keepdims=True) + 1e-09)
        out = jnp.einsum('bsk,bskh->bsh', w, out_k)
        return out

    def _L1_gnn_ref(x, W1, b1, W2, b2, edge_index):
        import jax, jax.numpy as jnp
        import numpy as np
        N_NODES = 1250
        D = 768
        N_EDGES = 20000

        def gcn_conv(x, W, b, src, dst, n_nodes):
            h = x @ W
            deg = jax.ops.segment_sum(jnp.ones_like(dst, dtype=h.dtype), dst, num_segments=n_nodes)
            dinv = jnp.where(deg > 0, jax.lax.rsqrt(deg), 0.0)
            norm = dinv[src] * dinv[dst]
            msgs = h[src] * norm[:, None]
            out = jax.ops.segment_sum(msgs, dst, num_segments=n_nodes)
            return out + b

        def add_self_loops(edge_index, n_nodes):
            loop = jnp.arange(n_nodes, dtype=edge_index.dtype)
            src = jnp.concatenate([edge_index[0], loop])
            dst = jnp.concatenate([edge_index[1], loop])
            return (src, dst)
        n = x.shape[0]
        src, dst = add_self_loops(edge_index, n)
        h = gcn_conv(x, W1, b1, src, dst, n)
        h = jax.nn.relu(h)
        out = gcn_conv(h, W2, b2, src, dst, n)
        return out

    def _L1_mix_ref(x, w_qkv, w_proj, b_proj):
        import jax, jax.numpy as jnp
        import numpy as np
        NUM_HEADS = 12

        def _l2_norm(t):
            return t / jnp.linalg.norm(t, axis=-2, keepdims=True)

        def _reference_tuple_inner(x, w_qkv, w_proj, b_proj):
            B, N, C = x.shape
            H = NUM_HEADS
            D = C // H
            qkv = (x @ w_qkv).reshape(B, N, 3, H, D).transpose(2, 0, 3, 1, 4)
            q, k, v = (qkv[0], qkv[1], qkv[2])
            q = _l2_norm(q)
            kT = _l2_norm(k).transpose(0, 1, 3, 2)
            sum_k = kT.sum(axis=-1)
            D_inv = 1.0 / (N + jnp.einsum('bhnd,bhd->bhd', q, sum_k))
            attn_matrix = jnp.einsum('bhnd,bhdn->bhdn', q, kT) * D_inv[..., None]
            matrix = jnp.einsum('bhnd,bhdn->bdhn', v, kT)
            y = jnp.einsum('bdhn,bhdn->bhnd', matrix, attn_matrix)
            y = y.transpose(0, 2, 1, 3).reshape(B, N, C)
            out = y @ w_proj + b_proj
            return (out, attn_matrix)
        return _reference_tuple_inner(x, w_qkv, w_proj, b_proj)[0]

    def _L1_ffn_ref(x, Wg, bg, W1, b1, W2, b2):
        import jax, jax.numpy as jnp
        import numpy as np
        B, T, D, H, E = (4, 256, 768, 384, 8)
        b, t, d = x.shape
        xf = x.reshape(-1, d)
        n = xf.shape[0]
        logits = xf @ Wg.T + bg
        probs = jax.nn.softmax(logits, axis=-1)
        top2_vals, top2_idx = jax.lax.top_k(probs, 2)
        cw = jnp.zeros((n, Wg.shape[0]), dtype=x.dtype)
        cw = cw.at[jnp.arange(n)[:, None], top2_idx].set(top2_vals)
        h = jax.nn.gelu(jnp.einsum('nd,edh->neh', xf, W1) + b1[None], approximate=False)
        y = jnp.einsum('neh,ehd->ned', h, W2) + b2[None]
        out = jnp.einsum('ne,ned->nd', cw, y)
        return out.reshape(b, t, d)
    edge_index = jnp.stack([src, dst])
    xn = _layernorm(x, axis=-1)
    x = x + _L0_gnn_ref(xn, src, dst, L0_gnn_W, L0_gnn_attn_l, L0_gnn_attn_r, L0_gnn_W_res) + _L0_mix_ref(xn[None], L0_mix_w_qkv, L0_mix_w_proj, L0_mix_b_proj)[0]
    x = x + _L0_ffn_ref(_layernorm(x, axis=-1)[None], L0_ffn_router_w, L0_ffn_router_b, L0_ffn_expert_w, L0_ffn_expert_b)[0]
    xn = _layernorm(x, axis=-1)
    x = x + _L1_gnn_ref(xn, L1_gnn_W1, L1_gnn_b1, L1_gnn_W2, L1_gnn_b2, edge_index) + _L1_mix_ref(xn[None], L1_mix_w_qkv, L1_mix_w_proj, L1_mix_b_proj)[0]
    x = x + _L1_ffn_ref(_layernorm(x, axis=-1)[None], L1_ffn_Wg, L1_ffn_bg, L1_ffn_W1, L1_ffn_b1, L1_ffn_W2, L1_ffn_b2)[0]
    return x

_drawn_inputs = setup_inputs


def setup_inputs(seed=0):
    import zlib

    import numpy as np

    out = dict(_drawn_inputs(seed))
    spreads = {'L0_mix_b_proj': (0.0, 0.1),
     'L1_gnn_b1': (0.0, 0.1),
     'L1_gnn_b2': (0.0, 0.1),
     'L1_mix_b_proj': (0.0, 0.1)}
    factors = {'L0_mix_w_qkv': 2.925,
     'L0_mix_w_proj': 3.207,
     'L0_ffn_expert_b': 4.194,
     'L1_mix_w_qkv': 8.0,
     'L1_mix_w_proj': 8.0,
     'L1_ffn_bg': 5.9,
     'L1_ffn_b1': 8.0,
     'L1_ffn_b2': 3.97}
    for name, (base, spread) in spreads.items():
        noise = np.random.default_rng([zlib.crc32(name.encode()), seed]).standard_normal(out[name].shape)
        drawn = base * np.exp(spread * noise) if base else spread * noise
        out[name] = jnp.asarray(drawn.astype(out[name].dtype))
    for name, factor in factors.items():
        out[name] = (out[name] * factor).astype(out[name].dtype)
    return out
```

```python
import concourse.bass as bass
from concourse import mybir

F32 = mybir.dt.float32
FR = mybir.dt.float32r
BF16 = mybir.dt.bfloat16
F16 = mybir.dt.float16
I32 = mybir.dt.int32
ALU = mybir.AluOpType
ACT = mybir.ActivationFunctionType
AX = mybir.AxisListType

P = 128
N = 1250
NT, T = 10, 125
C = 768
KC = C // P
E = 20000
ET = E // T
H, D = 12, 64
NP = H // 2
DW = D + 2
NE = 8
FH = 384
CH = [(0, 418), (418, 416), (834, 416)]
HC = C // 2
LN_EPS = 1e-5
SLOPE = 0.2
TINY = 1e-37
SLOTS = 4
BSLOTS = 4
RH = N // 2
STOP = 99


class Jobs:

    def __init__(self):
        self.owner, self.at = [], {}

    def add(self, name, owners):
        self.at[name] = len(self.owner)
        self.owner += owners

    def filled(self, m):
        return sum(o is not None for o in self.owner[:m + 1])

    def emptied(self, who, m):
        return sum(o == who for o in self.owner[:m + 1])


def plan_jobs():
    j = Jobs()
    a, v = "act", "dve"
    j.add("edges", [v])
    j.add("lnt0", [a] * 20)
    j.add("kv", [v, v, a, a] * NT)
    j.add("kvsum", [v] * NP)
    j.add("q0", [v] * 18)
    j.add("lin", [v] * 36)
    j.add("proj0", [v] * 20)
    j.add("attn_vec", [v])
    j.add("node_att", [v])
    j.add("att_rows", [v] * 3)
    j.add("att_max", [v])
    for L in (1, 2, 3):
        j.add(f"lnt{L}", [a] * 20)
        if L in (1, 3):
            j.add(f"route{L}", [v])
            j.add(f"gatesT{L}", [a] * 3)
            j.add(f"ebias{L}", [v] * 20)
            j.add(f"pad{L}", [None] * (-len(j.owner) % 8))
            j.add(f"experts{L}", [v] * (20 * NE) if L == 1 else ([a] * 9 + [v] * 20 + [None] * 3) * NE)
        else:
            j.add("q1", [a] * 18)
            j.add("k1", [a] * 18)
            j.add("v1", [v] * 18)
            j.add("proj1", [v] * 20)
            j.add("deg", [v] * 3)
            j.add("dinv", [v] * 3)
            j.add("conv1", [a] * 20)
            j.add("agg1", [v] * 18)
            j.add("conv2", [a] * 20)
            j.add("agg2", [v] * 20)
    return j


def graph_transformer(nc, x, src, dst, gW, gWT, gWresT, attnT, w0, wp0, bp0, rwT, rb, ewT, eb,
                      W1, b1c, W2, b2, w1, wp1, bp1, fgT, fbg, fW1, fb1c, fW2, fb2, out):
    J = plan_jobs()

    cursor = [(nc.sbuf_base + 63) // 32 * 32]

    def sb(name, shape, dt=F32):
        n = 1
        for s in shape[1:]:
            n *= s
        n *= 2 if dt in (BF16, F16) else 4
        t = nc.alloc_sbuf_tensor_at(name, shape, dt, offset=cursor[0])
        cursor[0] += (n + 31) // 32 * 32
        return t[:]

    PS = nc.alloc_psum_tensor("PS", [P, 8, 512], F32)[:]

    X = sb("X", [T, NT, C])
    XT = sb("XT", [P, KC, N])
    at_base = cursor[0]
    AT = sb("AT", [T, NT, N], FR)
    ident = sb("ident", [P, P])
    ones = sb("ones", [P, P])
    onesr = sb("onesr", [P, P], FR)
    stats = sb("stats", [T, NT, 12])
    mv = sb("mv", [T, NT, 2])
    std = sb("std", [T, NT])
    rstd = sb("rstd", [T, NT])
    GT = sb("GT", [T, NT, 2 * H])
    GB = sb("GB", [T, H])
    EX = sb("EX", [T, 4, NT, H])
    vvn = sb("vvn", [P, 2 * H])
    pref = sb("pref", [T, NE])
    pref_i = sb("pref_i", [T, NE], I32)
    base = cursor[0]
    top = nc.sbuf_usable_end // 32 * 32
    cursor[0] = top - 2 * C * 4
    XN = sb("XN", [T, 2, C])
    cursor[0] = top - 2 * C * 4 - 8192
    EI = sb("EI", [80, 4, T], I32)
    EF = sb("EF", [80, 4, T])
    ES = sb("ES", [T, 2, ET])
    wide = sb("wide", [D, P])
    attn_sb = sb("attn_sb", [D, 2 * H])
    vv = sb("vv", [P, 2 * H])
    vz = sb("vz", [P, NP, 2 * H])
    assert cursor[0] <= top - 2 * C * 4

    cursor[0] = base
    WS = sb("WS", [P, 2, KC * C])
    small = cursor[0]
    VR = sb("VR", [T, NT, NP, P + 2])
    KVB = sb("KVB", [P, NP, P])
    KSB = sb("KSB", [P, NP, P])
    TK = sb("TK", [T, 2, 2, HC])
    assert cursor[0] <= top - 2 * C * 4 - 8192, cursor[0]
    cursor[0] = small
    QT = sb("QT", [P, KC, N])
    cursor[0] = at_base
    KR = sb("KR", [T, NT, C])
    TQ = sb("TQ", [P, 2, 2, 418])
    BB = sb("BB", [T, C])
    assert cursor[0] <= at_base + NT * N * 4

    cursor[0] = base
    ZZ = sb("ZZ", [T, 4, NT, H])
    iota = sb("iota", [P, N], F16)
    iota_i = sb("iota_i", [P, N], I32)
    OHS = sb("OHS", [T, SLOTS, N], BF16)
    OHD = sb("OHD", [T, SLOTS, T], BF16)
    zeros = sb("zeros", [T, 512], BF16)
    AROW = sb("AROW", [T, 2, N])
    gidx = sb("gidx", [80, 2, NT])
    gidx_i = sb("gidx_i", [80, 2, NT], I32)
    tidx = sb("tidx", [80, 2])
    tidx_i = sb("tidx_i", [80, 2], I32)
    mnx = sb("mnx", [80, 2, 2])
    hit = sb("hit", [80, 2, 2, NT])
    rng = sb("rng", [2 * NT, 1])
    span = sb("span", [1, 8, NT])
    table = sb("table", [1, 3, NT], I32)
    gmax = sb("gmax", [H, 4])
    gdiag = sb("gdiag", [H, H])
    assert cursor[0] <= top - 2 * C * 4 - 8192

    cursor[0] = base
    PF = sb("PF", [T, 2, NT, 2, 2 * DW], FR)
    B1 = sb("B1", [T, BSLOTS, RH], FR)
    XPS = sb("XPS", [P, N])
    VRS = sb("VRS", [P, 2, T])
    WBD = sb("WBD", [P, 2 * P])
    FT = sb("FT", [T, NT, 2, DW])
    RES = sb("RES", [T, 2, NT, P])
    F = sb("F", [T, NT, 2 * DW])
    A2B = sb("A2B", [T, 2, N])
    Y1 = sb("Y1", [T, 2, 5, 4 * DW])
    YA = sb("YA", [T, NT, 2, 2, DW])
    YT = sb("YT", [T, 5, 2 * DW])
    NUM = sb("NUM", [T, 2, 5, DW])
    RD = sb("RD", [T, 5, 1])

    cursor[0] = small
    RW = sb("RW", [P, KC, NE])
    RB = sb("RB", [T, NE])
    EB = sb("EB", [NE, C])
    GA = sb("GA", [T, NT, NE])
    RS = sb("RS", [T, 10, NT, NE])
    R1 = sb("R1", [T, 8, NT])
    WT = sb("WT", [NE, N])
    HB = sb("HB", [P, NE, FH // P])
    HBS = sb("HBS", [P, 2, FH // P])
    HE = sb("HE", [P, 2, FH // P, N])
    assert cursor[0] <= top - 2 * C * 4
    cursor[0] = small
    QK = sb("QK", [P, KC, N])
    K2 = sb("K2", [P, 2, 418])
    JK = sb("JK", [P, 2, 418])
    SQ = sb("SQ", [P, 4, KC, 3])
    S4 = sb("S4", [P, 4, KC])
    SC = sb("SC", [P, 6, KC])
    BB1 = sb("BB1", [T, 2, C])
    assert cursor[0] <= top - 2 * C * 4
    cursor[0] = base + KC * C * 4
    HH = sb("HH", [T, 2, NT, C], FR)
    HF = sb("HF", [T, 2, HC])
    DB = sb("DB", [P, N])
    DT = sb("DT", [T, NT])
    TA = sb("TA", [P, 2, 418])
    B1C = sb("B1C", [P, KC])

    sem = nc.alloc_semaphore
    x_in, e_in, gw_in, c_in = sem("x_in"), sem("e_in"), sem("gw_in"), sem("c_in")
    w_in = [sem("w_in0"), sem("w_in1")]
    consts = sem("consts")
    pe_filled, act_emptied, dve_emptied = sem("pe_filled"), sem("act_emptied"), sem("dve_emptied")
    ln_var, ln_std, xn_ready = sem("ln_var"), sem("ln_std"), sem("xn_ready")
    wide_ready, edge_f, ranged, table_ready = sem("wide_ready"), sem("edge_f"), sem("ranged"), sem("table_ready")
    oh_ready, oh_free, acc_done, arow_ready, tr_filled, tr_emptied = (sem(s) for s in (
        "oh_ready", "oh_free", "acc_done", "arow_ready", "tr_filled", "tr_emptied"))
    vz_ready, gdiag_ready, z_ready, e_ready = sem("vz_ready"), sem("gdiag_ready"), sem("z_ready"), sem("e_ready")
    wbd_ready, wbd_zero, vrs_ready = sem("wbd_ready"), sem("wbd_zero"), sem("vrs_ready")
    xp_staged, xp_used, g56_filled, g56_emptied = (sem(s) for s in ("xp_staged", "xp_used", "g56_filled", "g56_emptied"))
    a2_filled, a2_emptied = sem("a2_filled"), sem("a2_emptied")
    f_ready, pf_hi, pf_ready = sem("f_ready"), sem("pf_hi"), sem("pf_ready")
    b1_ready, b1_used, accb_filled, y_emptied, y_used, pool_step, num_ready, num_used = (sem(s) for s in (
        "b1_ready", "b1_used", "accb_filled", "y_emptied", "y_used", "pool_step", "num_ready", "num_used"))
    kexp, qexp, kvb_zero = sem("kexp"), sem("qexp"), sem("kvb_zero")
    gexp_in, gexp_out, gates_ready = sem("gexp_in"), sem("gexp_out"), sem("gates_ready")
    w_used, sum_step = sem("w_used"), sem("sum_step")
    k2_ready, k2_used, deg_sum, deg_root, hf_hi, hf_used, h1_ready, loops = (sem(s) for s in (
        "k2_ready", "k2_used", "deg_sum", "deg_root", "hf_hi", "hf_used", "h1_ready", "loops"))
    norm_in, norm_out = sem("norm_in"), sem("norm_out")
    mix_bias, small_in, done, stored = sem("mix_bias"), sem("small_in"), sem("done"), sem("stored")
    misc_in = sem("misc_in")
    stage_done = sem("stage_done")

    W3 = [WS[:, s, :].rearrange("p (k c) -> p k c", k=KC) for s in range(2)]

    def bank(m):
        return PS[:, m % 8, :]

    block_ctx = nc.Block()
    block = block_ctx.__enter__()

    units = [("w0", 1), ("w0", 2), ("w0", 0), ("wp0", 0)] + [("ew", e) for e in range(NE)] \
        + [("w1", 0), ("w1", 1), ("w1", 2), ("wp1", 0), ("W1", 0), ("W2", 0)] + [("ff", e) for e in range(NE)]
    U_EW, U_MIX1, U_GCN, U_FF = 4, 12, 16, 18
    slot_of = [u % 2 if u < U_GCN or u >= U_FF else 0 for u in range(len(units))]
    copies = [2 if kind == "ff" else 1 for kind, e in units]

    def arrived(u):
        return 16 * sum(copies[v] for v in range(u + 1) if slot_of[v] == slot_of[u])

    last = lambda name, n: J.at[name] + n - 1
    used = [last("kv", 40), last("kv", 40), last("q0", 18), last("proj0", 20)] \
        + [last("experts1", 20 * (e + 1)) for e in range(NE)] \
        + [last("q1", 18), last("k1", 18), last("v1", 18), last("proj1", 20), last("conv1", 20), last("conv2", 20)] \
        + [last("experts3", 32 * (e + 1)) for e in range(NE)]

    @block.sync
    def _(sp):
        sp.dma_start(X, x.rearrange("(t p) c -> p t c", p=T)).then_inc(x_in, 16)
        sp.dma_start(EI[:, 0:2, :], src.rearrange("(a p e) -> p a e", a=2, p=80)).then_inc(e_in, 16)
        sp.dma_start(EI[:, 2:4, :], dst.rearrange("(a p e) -> p a e", a=2, p=80)).then_inc(e_in, 16)

        def load(u):
            kind, e = units[u]
            s = slot_of[u]
            if kind in ("w0", "w1"):
                w = (w0 if kind == "w0" else w1).rearrange("(k p) n -> p k n", p=P)
                sp.dma_start(W3[s], w[:, :, e * C:(e + 1) * C]).then_inc(w_in[s], 16)
            elif kind == "ff":
                sp.dma_start(WS[:, s, 0:KC * FH].rearrange("p (k h) -> p k h", k=KC),
                             fW1[e].rearrange("(k p) h -> p k h", p=P)).then_inc(w_in[s], 16)
                sp.dma_start(WS[:, s, KC * FH:].rearrange("p (k h) -> p k h", k=FH // P),
                             fW2[e].rearrange("(k p) h -> p k h", p=P)).then_inc(w_in[s], 16)
            else:
                w = {"wp0": wp0, "wp1": wp1, "W1": W1, "W2": W2}.get(kind)
                w = ewT[e] if w is None else w
                sp.dma_start(W3[s], w.rearrange("(k p) n -> p k n", p=P)).then_inc(w_in[s], 16)

        def unit_left(u):
            sp.wait_ge(pe_filled, J.filled(used[u]))

        load(0)
        load(1)
        sp.dma_start(wide[:, 0:D], gW).then_inc(gw_in, 16)
        sp.dma_start(wide[:, D:P], gW).then_inc(gw_in, 16)
        sp.dma_start(attn_sb, attnT).then_inc(gw_in, 16)
        sp.dma_start(BB, bp0.partition_broadcast(T)).then_inc(mix_bias, 16)
        for u in (2, 3):
            unit_left(u - 2)
            load(u)
        sp.wait_ge(wbd_zero, 1)
        for o in (0, D):
            sp.dma_start(WBD[o:o + D, o:o + D], gWT).then_inc(wbd_ready, 16)
            sp.dma_start(WBD[o:o + D, P + o:P + o + D], gWresT).then_inc(wbd_ready, 16)
        if STOP <= 1:
            sp.wait_ge(done, 1)
            sp.dma_start(out.rearrange("(t p) c -> p t c", p=T), X).then_inc(stored, 16)
            sp.wait_ge(stored, 16)
            return
        sp.wait_ge(stage_done, 1)
        load(U_EW)
        load(U_EW + 1)
        sp.dma_start(RW, rwT.rearrange("(k p) e -> p k e", p=P)).then_inc(small_in, 16)
        sp.dma_start(RB, rb.partition_broadcast(T)).then_inc(small_in, 16)
        sp.dma_start(EB, eb).then_inc(small_in, 16)
        for u in range(U_EW + 2, U_MIX1 + 2 if STOP > 3 else U_MIX1):
            unit_left(u - 2)
            load(u)
        if STOP > 3:
            sp.wait_ge(stage_done, 2)
            sp.dma_start(BB1[:, 0, :], b2.partition_broadcast(T)).then_inc(mix_bias, 16)
            sp.dma_start(BB1[:, 1, :], bp1.partition_broadcast(T)).then_inc(mix_bias, 16)
            for u in range(U_MIX1 + 2, U_GCN + 1):
                unit_left(u - 2)
                load(u)
            sp.wait_ge(stage_done, 3)
            sp.dma_start(B1C, b1c).then_inc(misc_in, 16)
            unit_left(U_GCN)
            load(U_GCN + 1)
        if STOP > 4:
            unit_left(U_GCN + 1)
            load(U_FF)
            sp.wait_ge(stage_done, 4)
            load(U_FF + 1)
            sp.dma_start(RW, fgT.rearrange("(k p) e -> p k e", p=P)).then_inc(small_in, 16)
            sp.dma_start(RB, fbg.partition_broadcast(T)).then_inc(small_in, 16)
            sp.dma_start(EB, fb2).then_inc(small_in, 16)
            sp.dma_start(HB, fb1c).then_inc(small_in, 16)
            for u in range(U_FF + 2, len(units)):
                unit_left(u - 2)
                load(u)
        sp.wait_ge(done, 1)
        sp.dma_start(out.rearrange("(t p) c -> p t c", p=T), X).then_inc(stored, 16)
        sp.wait_ge(stored, 16)

    @block.gpsimd
    def _(pool):
        nc.gpsimd.memset(ident, 0.0).then_inc(pool_step, 1)
        pool.wait_ge(pool_step, 1)
        nc.gpsimd.affine_select(out=ident, in_=ident, compare_op=ALU.not_equal, fill=1.0, base=0,
                                pattern=[[-1, P]], channel_multiplier=1).then_inc(consts, 1)
        nc.gpsimd.iota(pref_i, pattern=[[-1, NE]], base=NE, channel_multiplier=0).then_inc(consts, 1)
        pool.wait_ge(pe_filled, J.filled(J.at["proj0"] + 19))
        nc.gpsimd.iota(iota_i, pattern=[[1, N]], base=0, channel_multiplier=0).then_inc(consts, 1)
        nc.gpsimd.iota(gidx_i, pattern=[[T, 2], [T, NT]], base=0, channel_multiplier=0).then_inc(consts, 1)
        nc.gpsimd.iota(tidx_i, pattern=[[80, 2]], base=0, channel_multiplier=1).then_inc(consts, 1)
        steps = [1]

        def combine(i, g):
            j, half = g // 2, g % 2
            h = i * 2 + j
            t0 = half * 5
            y = Y1[:, g % 2]
            n0 = 1 + 4 * (i * 4 + g)
            if g or not isinstance(i, int):
                pool.wait_ge(num_ready, i * 4 + g)
            pool.wait_ge(y_emptied, i * 20 + 5 * (g + 1))
            pool.wait_ge(g56_emptied, i * 15 + 15)
            if g >= 2 or not isinstance(i, int):
                pool.wait_ge(num_used, i * 4 + g - 1)
            z = NUM[:, g % 2]
            nc.gpsimd.tensor_tensor(YT, y[:, :, 0:2 * DW], y[:, :, 2 * DW:], ALU.add).then_inc(y_used, 1)
            nc.gpsimd.tensor_tensor(z, YA[:, t0:t0 + 5, j, 0, :], YA[:, t0:t0 + 5, j, 1, :], ALU.add).then_inc(pool_step, 1)
            pool.wait_ge(y_used, i * 4 + g + 1)
            pool.wait_ge(pool_step, n0 + 1)
            nc.gpsimd.tensor_tensor(z, z, YT[:, :, DW:], ALU.subtract).then_inc(pool_step, 1)
            q1 = EX[:, 2, t0:t0 + 5, bass.ds(h, 1)].to_broadcast([T, 5, DW])
            q2 = EX[:, 3, t0:t0 + 5, bass.ds(h, 1)].to_broadcast([T, 5, DW])
            pool.wait_ge(pool_step, n0 + 2)
            nc.gpsimd.tensor_tensor(z, z, q2, ALU.mult).then_inc(pool_step, 1)
            nc.gpsimd.tensor_tensor(YT[:, :, 0:DW], YT[:, :, 0:DW], q1, ALU.mult).then_inc(pool_step, 1)
            pool.wait_ge(pool_step, n0 + 4)
            nc.gpsimd.tensor_tensor(z, z, YT[:, :, 0:DW], ALU.add).then_inc(num_ready, 1)

        if STOP >= 1:
            pool.wait_ge(e_ready, 4)
            for g in range(4):
                combine(0, g)
            with nc.gpsimd.Fori(1, NP) as i:
                for g in range(4):
                    combine(i, g)

    @block.tensor
    def _(pe):
        def begin(m):
            for k in range(m - 8, -1, -1):
                if k % 8 == m % 8 and J.owner[k]:
                    pe.wait_ge(act_emptied if J.owner[k] == "act" else dve_emptied, J.emptied(J.owner[k], k))
                    break
            return bank(m)

        def transposes(L):
            m0 = J.at[f"lnt{L}"]
            for t in range(NT):
                pe.wait_ge(xn_ready, L * NT + t + 1)
                for b in range(2):
                    ps = begin(m0 + 2 * t + b)
                    for k in range(3):
                        last = nc.tensor.transpose(ps[:, k * T:(k + 1) * T],
                                                   XN[:, t % 2, (3 * b + k) * P:(3 * b + k + 1) * P], ident[0:T, 0:T])
                    last.then_inc(pe_filled, 1)

        def xt_ready(L):
            m = J.at[f"lnt{L}"] + 19
            pe.wait_ge(act_emptied, J.emptied("act", m))

        def weights(u):
            pe.wait_ge(w_in[slot_of[u]], arrived(u))
            return W3[slot_of[u]]

        def rows(m0, lhsT, w, t, halves=2, last_inc=None):
            for b in range(halves):
                ps = begin(m0 + b)
                for k in range(KC):
                    last = nc.tensor.matmul(ps[0:T, 0:HC], lhsT[:, k, t * T:(t + 1) * T], w[:, k, b * HC:(b + 1) * HC],
                                            start=(k == 0), stop=(k == KC - 1))
                last.then_inc(pe_filled, 1)

        def columns(m0, w, rhs):
            for q in range(KC):
                for c, (o, n) in enumerate(CH):
                    ps = begin(m0 + 3 * q + c)
                    for k in range(KC):
                        last = nc.tensor.matmul(ps[:, 0:n], w[:, k, q * P:(q + 1) * P], rhs[:, k, o:o + n],
                                                start=(k == 0), stop=(k == KC - 1))
                    last.then_inc(pe_filled, 1)

        pe.wait_ge(consts, 1)
        pe.wait_ge(edge_f, 1)
        ps = begin(0)
        for k in range(4):
            last = nc.tensor.transpose(ps[0:T, k * 80:(k + 1) * 80], EF[:, k, :], ident[0:80, 0:80])
        last.then_inc(pe_filled, 1)
        transposes(0)
        xt_ready(0)
        wk, wv = weights(0), weights(1)
        for t in range(NT):
            m = J.at["kv"] + 4 * t
            rows(m, XT, wk, t)
            rows(m + 2, XT, wv, t)
        pe.wait_ge(dve_emptied, J.emptied("dve", J.at["kvsum"] - 1))
        pe.wait_ge(act_emptied, J.emptied("act", J.at["kvsum"] - 1))
        for p in range(NP):
            ps = begin(J.at["kvsum"] + p)
            for t in range(NT):
                last = nc.tensor.matmul(ps[:, 0:P + 2], KR[:, t, p * P:(p + 1) * P], VR[:, t, p, :],
                                        start=(t == 0), stop=(t == NT - 1))
            last.then_inc(pe_filled, 1)
        columns(J.at["q0"], weights(2), XT)
        for p in range(NP):
            for c, (o, n) in enumerate(CH):
                m = J.at["lin"] + 6 * p + 2 * c
                pe.wait_ge(dve_emptied, J.emptied("dve", J.at["q0"] + 3 * p + c))
                nc.tensor.matmul(begin(m)[:, 0:n], KSB[:, p, :], QT[:, p, o:o + n], start=True, stop=True).then_inc(pe_filled, 1)
                nc.tensor.matmul(begin(m + 1)[:, 0:n], KVB[:, p, :], QT[:, p, o:o + n], start=True, stop=True).then_inc(pe_filled, 1)
        w = weights(3)
        pe.wait_ge(dve_emptied, J.emptied("dve", J.at["proj0"] - 1))
        for t in range(NT):
            rows(J.at["proj0"] + 2 * t, QT, w, t)
        pe.wait_ge(gw_in, 48)
        ps = begin(J.at["attn_vec"])
        nc.tensor.matmul(ps[:, 0:2 * H], wide, attn_sb, start=True, stop=True).then_inc(pe_filled, 1)
        xt_ready(0)
        pe.wait_ge(vz_ready, 1)
        ps = begin(J.at["node_att"])
        for t in range(NT):
            for k in range(KC):
                last = nc.tensor.matmul(ps[0:T, t * 2 * H:(t + 1) * 2 * H], XT[:, k, t * T:(t + 1) * T], vz[:, k, :],
                                        start=(k == 0), stop=(k == KC - 1))
        last.then_inc(pe_filled, 1)
        for c, (o, n) in enumerate(CH):
            ps = begin(J.at["att_rows"] + c)
            for k in range(KC):
                last = nc.tensor.matmul(ps[0:H, 0:n], vz[:, k, 0:H], XT[:, k, o:o + n], start=(k == 0), stop=(k == KC - 1))
            last.then_inc(pe_filled, 1)
        pe.wait_ge(gdiag_ready, 1)
        ps = begin(J.at["att_max"])
        nc.tensor.matmul(ps[0:T, 0:H], ones[0:H, 0:T], gdiag, start=True, stop=True).then_inc(pe_filled, 1)

        pe.wait_ge(ranged, 1)
        pe.wait_ge(dve_emptied, J.emptied("dve", J.at["att_max"]))
        ps = PS[:, 7, :]
        for a in range(2):
            last = nc.tensor.transpose(ps[0:2 * NT, a * 80:(a + 1) * 80], hit[:, a, :, :].rearrange("p a b -> p (a b)"),
                                       ident[0:80, 0:80])
        last.then_inc(tr_filled, 1)
        pe.wait_ge(ranged, 2)
        nc.tensor.transpose(ps[0:1, 256:256 + 2 * NT], rng, ident[0:2 * NT, 0:2 * NT]).then_inc(tr_filled, 1)
        pe.wait_ge(table_ready, 1)

        def spread(g):
            pe.wait_ge(arow_ready, 3 * (g + 1))
            for q in range(3):
                r = 3 * g + q
                if r >= 2:
                    pe.wait_ge(tr_emptied, r - 1)
                for k in range(4 * q, min(4 * q + 4, NT)):
                    last = nc.tensor.transpose(PS[0:T, 6 + r % 2, (k % 4) * T:(k % 4 + 1) * T],
                                               AROW[:, g % 2, k * T:(k + 1) * T], ident[0:T, 0:T])
                last.then_inc(tr_filled, 1)

        for g in range(NT):
            n = nc.tensor.value_load(table[0:1, 1, g:g + 1], min_val=1, max_val=ET)
            done_before = nc.tensor.value_load(table[0:1, 2, g:g + 1], min_val=0, max_val=ET * NT)
            if g >= 2:
                pe.wait_ge(arow_ready, 3 * (g - 1))
            for c, (o, w) in enumerate(CH):
                nc.tensor.matmul(PS[0:T, 3 * (g % 2) + c, 0:w], zeros[:, 0:T], zeros[:, 0:w], start=True, stop=True)
            with nc.tensor.Fori(0, n) as j:
                u = done_before + j
                pe.wait_ge(oh_ready, u + 1)
                slot = u % SLOTS
                for c, (o, w) in enumerate(CH):
                    last = nc.tensor.matmul(PS[0:T, 3 * (g % 2) + c, 0:w],
                                            OHD[:, bass.ds(slot, 1), :].rearrange("p a b -> p (a b)"),
                                            OHS[:, bass.ds(slot, 1), o:o + w].rearrange("p a b -> p (a b)"),
                                            start=False, stop=True, skip_group_check=True)
                last.then_inc(oh_free, 1)
            nc.tensor.matmul(PS[0:T, 3 * (g % 2) + 2, 0:16], zeros[:, 0:T], zeros[:, 0:16], start=False, stop=True,
                             skip_group_check=True).then_inc(acc_done, 1)
            if g >= 1:
                spread(g - 1)
        spread(NT - 1)
        if STOP <= 0:
            return

        pe.wait_ge(wbd_ready, 64)
        pe.wait_ge(tr_emptied, 3 * NT)

        def pair(i):
            first = isinstance(i, int)
            pe.wait_ge(xp_staged, i + 1)
            for r in range(5):
                if r >= 2:
                    pe.wait_ge(g56_emptied, i * 15 + r - 1)
                else:
                    pe.wait_ge(g56_emptied, i * 15)
                for k in range(2):
                    last = nc.tensor.matmul(PS[0:T, 5 + r % 2, k * 256:(k + 1) * 256],
                                            XPS[:, (2 * r + k) * T:(2 * r + k + 1) * T], WBD, start=True, stop=True)
                last.then_inc(g56_filled, 1)
            pe.wait_ge(vrs_ready, i * 2 + 2)
            for j in range(2):
                for c, (o, n) in enumerate(CH):
                    r = 3 * j + c
                    if not first or r:
                        pe.wait_ge(a2_emptied, i * 6 + r)
                    last = nc.tensor.matmul(PS[0:T, 7, 0:n], VRS[:, j, :], XPS[:, o:o + n], start=True, stop=True)
                    last.then_inc(a2_filled, 1)
            pe.wait_ge(pf_ready, i * 2 + 2)
            for r in range(NT):
                pe.wait_ge(g56_emptied, i * 15 + 5 + r - 1)
                b = 5 + (r + 1) % 2
                for s in range(NT):
                    last = nc.tensor.matmul(PS[0:T, b, 0:4 * DW], AT[:, s, r * T:(r + 1) * T], PF[:, :, s, :, DW:],
                                            start=(s == 0), stop=(s == NT - 1))
                last.then_inc(g56_filled, 1)
            for g in range(4):
                j, half = g // 2, g % 2
                for s in range(NT):
                    pe.wait_ge(b1_ready, i * 40 + g * 10 + s + 1)
                    for b in range(5):
                        if s == 0 and (g or not first):
                            pe.wait_ge(y_emptied, i * 20 + 5 * (g - 1) + b + 1 if g else i * 20)
                        last = nc.tensor.matmul(PS[0:T, b, 0:4 * DW], B1[:, (g * 10 + s) % BSLOTS, b * T:(b + 1) * T],
                                                PF[:, j, s, :, :].rearrange("p a b -> p (a b)"),
                                                start=(s == 0), stop=(s == NT - 1))
                        if s == NT - 1 and b < 4:
                            last.then_inc(accb_filled, 1)
                    if s == NT - 1:
                        last.then_inc(accb_filled, 1)
                    else:
                        last.then_inc(b1_used, 1)

        pair(0)
        with nc.tensor.Fori(1, NP) as i:
            pair(i)
        if STOP <= 1:
            return
        pe.wait_ge(y_emptied, 20 * NP)
        pe.wait_ge(g56_emptied, 15 * NP)
        pe.wait_ge(a2_emptied, 6 * NP)

        def route(L):
            xt_ready(L)
            pe.wait_ge(small_in, 48 if L == 1 else 48 + 64)
            ps = begin(J.at[f"route{L}"])
            for t in range(NT):
                for k in range(KC):
                    last = nc.tensor.matmul(ps[0:T, t * NE:(t + 1) * NE], XT[:, k, t * T:(t + 1) * T], RW[:, k, :],
                                            start=(k == 0), stop=(k == KC - 1))
            last.then_inc(pe_filled, 1)
            pe.wait_ge(gates_ready, 1 if L == 1 else 2)
            for q in range(3):
                ps = begin(J.at[f"gatesT{L}"] + q)
                for t in range(4 * q, min(4 * q + 4, NT)):
                    last = nc.tensor.transpose(ps[0:NE, (t % 4) * T:(t % 4 + 1) * T], GA[:, t, :], ident[0:T, 0:T])
                last.then_inc(pe_filled, 1)
            pe.wait_ge(act_emptied, J.emptied("act", J.at[f"gatesT{L}"] + 2))
            for t in range(NT):
                for b in range(2):
                    ps = begin(J.at[f"ebias{L}"] + 2 * t + b)
                    nc.tensor.matmul(ps[0:T, 0:HC], WT[:, t * T:(t + 1) * T], EB[:, b * HC:(b + 1) * HC],
                                     start=True, stop=True).then_inc(pe_filled, 1)
            m = J.at[f"experts{L}"] - 1
            pe.wait_ge(act_emptied, J.emptied("act", m))
            pe.wait_ge(dve_emptied, J.emptied("dve", m))

        transposes(1)
        route(1)
        d0 = J.emptied("dve", J.at["experts1"] - 1)
        with nc.tensor.Fori(0, NE // 2) as i:
            for e in range(2):
                pe.wait_ge(w_in[e], i * 16 + arrived(U_EW + e))
                for t in range(NT):
                    for b in range(2):
                        r = 20 * e + 2 * t + b
                        pe.wait_ge(dve_emptied, i * 40 + d0 + r - 7)
                        ps = bank(r)
                        for k in range(KC):
                            last = nc.tensor.matmul(ps[0:T, 0:HC], XT[:, k, t * T:(t + 1) * T],
                                                    W3[e][:, k, b * HC:(b + 1) * HC], start=(k == 0), stop=(k == KC - 1))
                        last.then_inc(pe_filled, 1)
        if STOP <= 3:
            return

        transposes(2)
        xt_ready(2)
        for n, name in enumerate(("q1", "k1", "v1")):
            columns(J.at[name], weights(U_MIX1 + n), XT)
        w = weights(U_MIX1 + 3)
        pe.wait_ge(dve_emptied, J.emptied("dve", J.at["proj1"] - 1))
        for t in range(NT):
            rows(J.at["proj1"] + 2 * t, QK, w, t)

        pe.wait_ge(loops, 1)
        for c, (o, n) in enumerate(CH):
            ps = begin(J.at["deg"] + c)
            for s in range(NT):
                last = nc.tensor.matmul(ps[:, 0:n], onesr[0:T, :], AT[:, s, o:o + n], start=(s == 0), stop=(s == NT - 1))
            last.then_inc(pe_filled, 1)
        pe.wait_ge(deg_root, 2)
        for q in range(3):
            ps = begin(J.at["dinv"] + q)
            for t in range(4 * q, min(4 * q + 4, NT)):
                last = nc.tensor.transpose(ps[0:T, (t % 4) * P:(t % 4 + 1) * P], DB[:, t * T:(t + 1) * T], ident)
            last.then_inc(pe_filled, 1)
        w = weights(U_GCN)
        for t in range(NT):
            rows(J.at["conv1"] + 2 * t, XT, w, t)
        pe.wait_ge(hf_hi, 20)
        pe.wait_ge(hf_used, 20)
        for q in range(KC):
            for c, (o, n) in enumerate(CH):
                ps = begin(J.at["agg1"] + 3 * q + c)
                for s in range(NT):
                    for v in range(2):
                        last = nc.tensor.matmul(ps[:, 0:n], HH[:, v, s, q * P:(q + 1) * P], AT[:, s, o:o + n],
                                                start=(s + v == 0), stop=(s == NT - 1 and v == 1))
                last.then_inc(pe_filled, 1)
        w = weights(U_GCN + 1)
        pe.wait_ge(h1_ready, 18)
        for t in range(NT):
            rows(J.at["conv2"] + 2 * t, XT, w, t)
        pe.wait_ge(hf_used, 40)
        for t in range(NT):
            for b in range(2):
                ps = begin(J.at["agg2"] + 2 * t + b)
                for s in range(NT):
                    for v in range(2):
                        last = nc.tensor.matmul(ps[0:T, 0:HC], AT[:, s, t * T:(t + 1) * T],
                                                HH[:, v, s, b * HC:(b + 1) * HC],
                                                start=(s + v == 0), stop=(s == NT - 1 and v == 1))
                last.then_inc(pe_filled, 1)
        if STOP <= 4:
            return

        transposes(3)
        route(3)
        m = J.at["experts3"] - 1
        a0, d0 = J.emptied("act", m), J.emptied("dve", m)
        with nc.tensor.Fori(0, NE // 2) as i:
            for e in range(2):
                wa = WS[:, e, 0:KC * FH].rearrange("p (k h) -> p k h", k=KC)
                wb = WS[:, e, KC * FH:].rearrange("p (k h) -> p k h", k=FH // P)
                pe.wait_ge(w_in[e], i * 32 + arrived(U_FF + e))
                for q in range(3):
                    for c, (o, n) in enumerate(CH):
                        r = 3 * q + c
                        if r < 5:
                            pe.wait_ge(dve_emptied, i * 40 + d0 + 20 * e - 4 + r if r < 4 else i * 40 + d0 + 20 * e)
                        if r == 8:
                            pe.wait_ge(act_emptied, i * 18 + a0 + 9 * e + 1)
                        ps = bank(r)
                        for k in range(KC):
                            last = nc.tensor.matmul(ps[:, 0:n], wa[:, k, q * P:(q + 1) * P], XT[:, k, o:o + n],
                                                    start=(k == 0), stop=(k == KC - 1))
                        last.then_inc(pe_filled, 1)
                pe.wait_ge(act_emptied, i * 18 + a0 + 9 * e + 9)
                for t in range(NT):
                    for b in range(2):
                        r = 2 * t + b
                        if r >= 8:
                            pe.wait_ge(dve_emptied, i * 40 + d0 + 20 * e + r - 7)
                        ps = bank(9 + r)
                        for k in range(FH // P):
                            last = nc.tensor.matmul(ps[0:T, 0:HC], HE[:, e, k, t * T:(t + 1) * T],
                                                    wb[:, k, b * HC:(b + 1) * HC], start=(k == 0), stop=(k == FH // P - 1))
                        last.then_inc(pe_filled, 1)

    @block.scalar
    def _(act):
        def full(m):
            act.wait_ge(pe_filled, J.filled(m))
            return bank(m)

        def transposed(L):
            act.wait_ge(ln_var, L + 1)
            nc.scalar.activation(std, std, ACT.Sqrt).then_inc(ln_std, 1)
            for t in range(NT):
                for b in range(2):
                    ps = full(J.at[f"lnt{L}"] + 2 * t + b)
                    nc.scalar.activation(XT[:, 3 * b:3 * b + 3, t * T:(t + 1) * T],
                                         ps[:, 0:3 * T].rearrange("p (k n) -> p k n", k=3), ACT.Copy).then_inc(act_emptied, 1)

        transposed(0)
        def lower_exp(tmp, ps, m_sem):
            nc.scalar.activation(tmp, ps, ACT.Relu, scale=-1.0)
            nc.scalar.drain()
            nc.scalar.activation(tmp, tmp, ACT.Exp, scale=-1.0).then_inc(m_sem, 1)

        for t in range(NT):
            for b in range(2):
                n = 2 * t + b
                ps = full(J.at["kv"] + 4 * t + b)
                if n >= 4:
                    act.wait_ge(dve_emptied, J.emptied("dve", J.at["kv"] + 4 * (t - 2) + b))
                lower_exp(TK[:, t % 2, b, :], ps[0:T, 0:HC], kexp)
            for b in range(2):
                ps = full(J.at["kv"] + 4 * t + 2 + b)
                nc.scalar.activation(VR[:, t, 3 * b:3 * b + 3, 0:P], ps[0:T, 0:HC].rearrange("p (k n) -> p k n", k=3),
                                     ACT.Copy).then_inc(act_emptied, 1)
        for r in range(18):
            n = CH[r % 3][1]
            ps = full(J.at["q0"] + r)
            if r >= 4:
                act.wait_ge(dve_emptied, J.emptied("dve", J.at["q0"] + r - 4))
            else:
                act.wait_ge(pe_filled, J.filled(J.at["kvsum"] + 5))
            lower_exp(TQ[:, r % 4 // 2, r % 2, 0:n], ps[:, 0:n], qexp)
        act.wait_ge(z_ready, 1)
        for f in range(4):
            nc.scalar.activation(EX[:, f], ZZ[:, f], ACT.Exp).then_inc(e_ready, 1)

        def turned(g):
            for q in range(3):
                r = 3 * g + q
                w = min(4 * q + 4, NT) - 4 * q
                act.wait_ge(tr_filled, 2 + r + 1)
                nc.scalar.activation(AT[:, 4 * q:4 * q + w, g * T:(g + 1) * T],
                                     PS[0:T, 6 + r % 2, 0:w * T].rearrange("p (s n) -> p s n", s=w),
                                     ACT.Copy).then_inc(tr_emptied, 1)

        for g in range(NT):
            act.wait_ge(acc_done, g + 1)
            if g >= 2:
                act.wait_ge(tr_filled, 2 + 3 * (g - 1))
            for c, (o, n) in enumerate(CH):
                nc.scalar.activation(AROW[:, g % 2, o:o + n], PS[0:T, 3 * (g % 2) + c, 0:n], ACT.Copy).then_inc(arow_ready, 1)
            if g >= 1:
                turned(g - 1)
        turned(NT - 1)
        if STOP <= 0:
            return

        def pair(i):
            first = isinstance(i, int)
            if not first:
                act.wait_ge(a2_filled, i * 6)
            nc.scalar.activation(XPS, XT[:, bass.ds(i, 1), :].rearrange("p a n -> p (a n)"), ACT.Copy).then_inc(xp_staged, 1)
            if not first:
                act.wait_ge(f_ready, i * 2)
            for r in range(5):
                act.wait_ge(g56_filled, i * 15 + r + 1)
                if r == 0 and not first:
                    act.wait_ge(num_used, i * 4 - 4)
                ps = PS[0:T, 5 + r % 2, :].rearrange("p (t c) -> p t c", t=2)
                for j in range(2):
                    nc.scalar.activation(FT[:, 2 * r:2 * r + 2, j, 0:D], ps[:, :, j * D:(j + 1) * D], ACT.Copy)
                nc.scalar.activation(RES[:, bass.ds(i % 2, 1), 2 * r:2 * r + 2, :].rearrange("p a t c -> p (a t) c"),
                                     ps[:, :, P:], ACT.Copy)
                nc.scalar.drain().then_inc(g56_emptied, 1)
            for j in range(2):
                if not first:
                    act.wait_ge(b1_ready, i * 40)
                for c, (o, n) in enumerate(CH):
                    act.wait_ge(a2_filled, i * 6 + 3 * j + c + 1)
                    nc.scalar.activation(A2B[:, j, o:o + n], PS[0:T, 7, 0:n], ACT.Copy).then_inc(a2_emptied, 1)
            for j in range(2):
                act.wait_ge(f_ready, i * 2 + j + 1)
                if not first:
                    act.wait_ge(accb_filled, i * 20)
                nc.scalar.activation(PF[:, j, :, 0, :], F, ACT.Copy).then_inc(pf_hi, 1)
            for r in range(NT):
                act.wait_ge(g56_filled, i * 15 + 5 + r + 1)
                if not first:
                    act.wait_ge(num_ready, i * 4)
                nc.scalar.activation(YA[:, r].rearrange("p a b c -> p (a b c)"), PS[0:T, 5 + (r + 1) % 2, 0:4 * DW],
                                     ACT.Copy).then_inc(g56_emptied, 1)
            for g in range(4):
                for b in range(5):
                    act.wait_ge(accb_filled, i * 20 + 5 * g + b + 1)
                    if b == 0 and (g >= 2 or not first):
                        act.wait_ge(y_used, i * 4 + g - 1)
                    nc.scalar.activation(Y1[:, g % 2, b, :], PS[0:T, b, 0:4 * DW], ACT.Copy).then_inc(y_emptied, 1)

        act.wait_ge(wbd_ready, 64)
        pair(0)
        with nc.scalar.Fori(1, NP) as i:
            pair(i)
        if STOP <= 1:
            return

        def route(L, k):
            act.wait_ge(gexp_in, k)
            nc.scalar.activation(RS[:, 1], RS[:, 0], ACT.Exp).then_inc(gexp_out, 1)
            for q in range(3):
                ps = full(J.at[f"gatesT{L}"] + q)
                w = (min(4 * q + 4, NT) - 4 * q) * T
                nc.scalar.activation(WT[:, 4 * q * T:4 * q * T + w], ps[0:NE, 0:w], ACT.Copy).then_inc(act_emptied, 1)

        transposed(1)
        route(1, 1)
        if STOP <= 3:
            return

        transposed(2)
        for r in range(18):
            q, c = r // 3, r % 3
            o, n = CH[c]
            ps = full(J.at["q1"] + r)
            nc.scalar.activation(QK[:, q, o:o + n], ps[:, 0:n], ACT.Copy, accum_out=SQ[:, 0, q, c:c + 1])
            nc.scalar.activation(JK[:, r % 2, 0:n], ps[:, 0:n], ACT.Square, accum_out=SQ[:, 2, q, c:c + 1])
            nc.scalar.drain().then_inc(act_emptied, 1)
        for r in range(18):
            q, c = r // 3, r % 3
            o, n = CH[c]
            ps = full(J.at["k1"] + r)
            if r >= 2:
                act.wait_ge(k2_used, r - 1)
            nc.scalar.activation(K2[:, r % 2, 0:n], ps[:, 0:n], ACT.Square, accum_out=SQ[:, 3, q, c:c + 1])
            nc.scalar.activation(JK[:, r % 2, 0:n], ps[:, 0:n], ACT.Copy, accum_out=SQ[:, 1, q, c:c + 1])
            nc.scalar.drain().then_inc(act_emptied, 1)
        act.wait_ge(norm_in, 1)
        nc.scalar.activation(SC[:, 0:2], S4[:, 2:4], ACT.Sqrt).then_inc(norm_out, 1)
        act.wait_ge(deg_sum, 1)
        nc.scalar.activation(DB, DB, ACT.Sqrt).then_inc(deg_root, 1)

        def scaled_rows(name, k):
            for r in range(20):
                t, b = r // 2, r % 2
                ps = full(J.at[name] + r)
                if 20 * k + r >= 2:
                    act.wait_ge(hf_used, 20 * k + r - 1)
                nc.scalar.activation(HF[:, b, :], ps[0:T, 0:HC], ACT.Copy, scale=DT[:, t:t + 1]).then_inc(act_emptied, 1)
                nc.scalar.drain()
                nc.scalar.activation(HH[:, 0, t, b * HC:(b + 1) * HC], HF[:, b, :], ACT.Copy).then_inc(hf_hi, 1)

        act.wait_ge(dve_emptied, J.emptied("dve", J.at["dinv"] + 2))
        scaled_rows("conv1", 0)
        act.wait_ge(misc_in, 16)
        for r in range(18):
            q, c = r // 3, r % 3
            o, n = CH[c]
            act.wait_ge(dve_emptied, J.emptied("dve", J.at["agg1"] + r))
            nc.scalar.activation(XT[:, q, o:o + n], TA[:, r % 2, 0:n], ACT.Relu, bias=B1C[:, q:q + 1]).then_inc(h1_ready, 1)
        scaled_rows("conv2", 1)
        if STOP <= 4:
            return

        transposed(3)
        route(3, 2)
        f0 = J.filled(J.at["experts3"] - 1)
        with nc.scalar.Fori(0, NE // 2) as i:
            for e in range(2):
                nc.scalar.activation(HBS[:, e, :], HB[:, bass.ds(i * 2 + e, 1), :].rearrange("p a b -> p (a b)"), ACT.Copy)
                nc.scalar.drain()
                for q in range(3):
                    for c, (o, n) in enumerate(CH):
                        r = 3 * q + c
                        act.wait_ge(pe_filled, i * 58 + f0 + 29 * e + r + 1)
                        nc.scalar.activation(HE[:, e, q, o:o + n], bank(r)[:, 0:n], ACT.Gelu,
                                             bias=HBS[:, e, q:q + 1]).then_inc(act_emptied, 1)

    @block.vector
    def _(dve):
        def full(m):
            dve.wait_ge(pe_filled, J.filled(m))
            return bank(m)

        V = nc.vector

        def layer_norm(L):
            for t in range(NT):
                for b in range(2):
                    V.bn_stats(stats[:, t, 6 * b:6 * b + 6], X[:, t, b * HC:(b + 1) * HC])
            V.drain()
            for t in range(NT):
                V.bn_aggr(mv[:, t, :], stats[:, t, :])
            V.drain()
            V.tensor_scalar(std, mv[:, :, 1], LN_EPS, None, ALU.add).then_inc(ln_var, 1)
            dve.wait_ge(ln_std, L + 1)
            V.reciprocal(rstd, std)
            V.drain()
            for t in range(NT):
                if t >= 2:
                    dve.wait_ge(pe_filled, J.filled(J.at[f"lnt{L}"] + 2 * (t - 2) + 1))
                V.tensor_scalar(XN[:, t % 2, :], X[:, t, :], mv[:, t, 0:1], rstd[:, t:t + 1], ALU.subtract,
                                ALU.mult).then_inc(xn_ready, 1)

        V.memset(ones, 1.0)
        V.drain()
        V.tensor_copy(onesr, ones)
        dve.wait_ge(e_in, 32)
        V.tensor_copy(EF, EI).then_inc(edge_f, 1)
        ps = full(0)
        V.tensor_copy(ES.rearrange("p a b -> p (a b)"), ps[0:T, 0:320]).then_inc(dve_emptied, 1)
        dve.wait_ge(x_in, 16)
        layer_norm(0)
        V.memset(VR[:, :, :, P:], 1.0)
        V.memset(KVB, 0.0)
        for t in range(NT):
            for b in range(2):
                n = 2 * t + b
                ps = full(J.at["kv"] + 4 * t + b)
                dve.wait_ge(kexp, n + 1)
                V.scalar_tensor_tensor(out=KR[:, t, b * HC:(b + 1) * HC], in0=ps[0:T, 0:HC], scalar=0.0,
                                       in1=TK[:, t % 2, b, :], op0=ALU.max, op1=ALU.add).then_inc(dve_emptied, 1)
        for p in range(NP):
            ps = full(J.at["kvsum"] + p)
            for r in range(2):
                rr = slice(r * D, (r + 1) * D)
                V.tensor_copy(KVB[rr, p, r * D:(r + 1) * D], ps[rr, r * D:(r + 1) * D])
                V.tensor_scalar(KSB[rr, p, :], ones[rr, :], ps[rr, P:P + 1], None, ALU.mult)
            V.drain()
            V.memset(KSB[0:D, p, D:], 0.0)
            V.memset(KSB[D:P, p, 0:D], 0.0)
            V.drain().then_inc(dve_emptied, 1)
        for r in range(18):
            o, n = CH[r % 3]
            ps = full(J.at["q0"] + r)
            dve.wait_ge(qexp, r + 1)
            V.scalar_tensor_tensor(out=QT[:, r // 3, o:o + n], in0=ps[:, 0:n], scalar=0.0, in1=TQ[:, r % 4 // 2, r % 2, 0:n],
                                   op0=ALU.max, op1=ALU.add).then_inc(dve_emptied, 1)
        V.drain()
        for r in range(18):
            p, c = r // 3, r % 3
            o, n = CH[c]
            m = J.at["lin"] + 2 * r
            ps = full(m)
            V.reciprocal(TQ[:, 0, r % 2, 0:n], ps[:, 0:n]).then_inc(dve_emptied, 1)
            ps = full(m + 1)
            V.drain()
            V.tensor_tensor(QT[:, p, o:o + n], ps[:, 0:n], TQ[:, 0, r % 2, 0:n], ALU.mult).then_inc(dve_emptied, 1)

        def add_rows(name, n=20):
            for r in range(n):
                t, b = r // 2, r % 2
                ps = full(J.at[name] + r)
                xs = X[:, t, b * HC:(b + 1) * HC]
                V.tensor_tensor(xs, ps[0:T, 0:HC], xs, ALU.add).then_inc(dve_emptied, 1)

        V.drain()
        add_rows("proj0")
        dve.wait_ge(mix_bias, 16)
        V.drain()
        V.tensor_tensor(X, X, BB.unsqueeze(1).to_broadcast([T, NT, C]), ALU.add)
        V.drain()
        V.memset(vz, 0.0)
        ps = full(J.at["attn_vec"])
        V.tensor_copy(vv, ps[:, 0:2 * H]).then_inc(dve_emptied, 1)
        V.drain()
        V.tensor_scalar(vvn, vv, -1.0, None, ALU.mult)
        vzf = vz.rearrange("p a b -> p (a b)")
        step = 2 * H + 2
        for side in range(2):
            for r in range(2):
                o = side * H + r
                V.tensor_copy(vzf[r * D:(r + 1) * D, o:o + 5 * step + 1:step], vv[r * D:(r + 1) * D, o:o + H - 1:2])
        V.drain().then_inc(vz_ready, 1)
        ps = full(J.at["node_att"])
        V.tensor_copy(GT.rearrange("p a b -> p (a b)"), ps[0:T, 0:NT * 2 * H]).then_inc(dve_emptied, 1)
        for c, (o, n) in enumerate(CH):
            ps = full(J.at["att_rows"] + c)
            V.tensor_reduce(gmax[:, c:c + 1], ps[0:H, 0:n], AX.X, ALU.max).then_inc(dve_emptied, 1)
        V.drain()
        V.tensor_reduce(gmax[:, 3:4], gmax[:, 0:3], AX.X, ALU.max)
        V.drain()
        V.tensor_scalar(gdiag, ident[0:H, 0:H], gmax[:, 3:4], None, ALU.mult).then_inc(gdiag_ready, 1)
        ps = full(J.at["att_max"])
        V.tensor_copy(GB, ps[0:T, 0:H]).then_inc(dve_emptied, 1)
        V.drain()
        gb = GB.unsqueeze(1).to_broadcast([T, NT, H])
        V.tensor_tensor(ZZ[:, 0], GT[:, :, 0:H], gb, ALU.subtract)
        V.tensor_tensor(ZZ[:, 2], GT[:, :, H:], gb, ALU.add)
        V.drain()
        V.tensor_scalar(ZZ[:, 1], ZZ[:, 0], SLOPE, None, ALU.mult)
        V.tensor_scalar(ZZ[:, 3], ZZ[:, 2], SLOPE - 1.0, 0.0, ALU.mult, ALU.min)
        V.drain()
        V.tensor_scalar(ZZ[:, 2], ZZ[:, 2], 1.0 - SLOPE, 0.0, ALU.mult, ALU.min)
        V.drain().then_inc(z_ready, 1)

        dve.wait_ge(consts, 5)
        V.tensor_copy(pref, pref_i)
        V.memset(zeros, 0.0)
        V.tensor_copy(iota, iota_i)
        V.tensor_copy(gidx, gidx_i)
        V.tensor_copy(tidx, tidx_i)
        for a in range(2):
            V.tensor_reduce(mnx[:, 0, a:a + 1], EF[:, 2 + a, :], AX.X, ALU.min)
            V.tensor_reduce(mnx[:, 1, a:a + 1], EF[:, 2 + a, :], AX.X, ALU.max)
        V.drain()
        for a in range(2):
            V.tensor_scalar(hit[:, a, 0, :], gidx[:, 0, :], mnx[:, 1, a:a + 1], None, ALU.is_le)
        V.drain()
        for a in range(2):
            V.scalar_tensor_tensor(out=hit[:, a, 1, :], in0=gidx[:, 1, :], scalar=mnx[:, 0, a:a + 1],
                                   in1=hit[:, a, 0, :], op0=ALU.is_gt, op1=ALU.mult)
        V.drain()
        V.tensor_scalar(mnx[:, 0, :], tidx, -1.0, float(ET), ALU.mult, ALU.add)
        V.tensor_scalar(mnx[:, 1, :], tidx, 1.0, None, ALU.add)
        V.drain()
        for a in range(2):
            V.tensor_scalar(hit[:, a, 0, :], hit[:, a, 1, :], mnx[:, 0, a:a + 1], None, ALU.mult)
        V.drain()
        for a in range(2):
            V.tensor_scalar(hit[:, a, 1, :], hit[:, a, 1, :], mnx[:, 1, a:a + 1], None, ALU.mult)
        V.drain().then_inc(ranged, 1)
        dve.wait_ge(tr_filled, 1)
        V.tensor_reduce(rng, PS[0:2 * NT, 7, 0:160], AX.X, ALU.max).then_inc(ranged, 1)
        dve.wait_ge(tr_filled, 2)
        V.tensor_copy(span[:, 0:2, :].rearrange("p a b -> p (a b)"), PS[0:1, 7, 256:256 + 2 * NT])
        V.drain()
        V.tensor_tensor(span[:, 3, :], span[:, 0, :], span[:, 1, :], ALU.add)
        V.tensor_scalar(span[:, 2, :], span[:, 0, :], -1.0, float(ET), ALU.mult, ALU.add)
        V.drain()
        V.tensor_scalar(span[:, 3, :], span[:, 3, :], float(-ET), 1.0, ALU.add, ALU.max)
        V.tensor_scalar(span[:, 2, :], span[:, 2, :], float(ET - 1), None, ALU.min)
        V.memset(span[:, 5, :], 0.0)
        V.drain()
        V.tensor_tensor_scan(out=span[:, 4, :], data0=span[:, 3, :], data1=span[:, 5, :], initial=0.0, op0=ALU.add, op1=ALU.add)
        V.drain()
        V.tensor_tensor(span[:, 4, :], span[:, 4, :], span[:, 3, :], ALU.subtract)
        V.drain()
        V.tensor_copy(table, span[:, 2:5, :])
        V.drain().then_inc(table_ready, 1)
        for g in range(NT):
            t0 = nc.vector.value_load(table[0:1, 0, g:g + 1], min_val=0, max_val=ET - 1)
            n = nc.vector.value_load(table[0:1, 1, g:g + 1], min_val=1, max_val=ET)
            done_before = nc.vector.value_load(table[0:1, 2, g:g + 1], min_val=0, max_val=ET * NT)
            if g == 0:
                nc.vector.engine_nop().then_inc(oh_free, SLOTS)
            with nc.vector.Fori(0, n) as j:
                u = done_before + j
                tile = nc.s_assert_within(t0 + j, 0, ET - 1, skip_runtime_bounds_check_because=
                                          "a span's first tile and length come from the same ET tiles")
                slot = u % SLOTS
                dve.wait_ge(oh_free, u + 1)
                V.tensor_scalar(OHS[:, bass.ds(slot, 1), :].rearrange("p a b -> p (a b)"), iota[0:T, :],
                                ES[:, 0, bass.ds(tile, 1)], None, ALU.is_equal)
                V.tensor_scalar(OHD[:, bass.ds(slot, 1), :].rearrange("p a b -> p (a b)"), iota[0:T, g * T:(g + 1) * T],
                                ES[:, 1, bass.ds(tile, 1)], None, ALU.is_equal)
                V.drain().then_inc(oh_ready, 1)
        dve.wait_ge(tr_filled, 2 + 3 * NT)
        V.memset(WBD, 0.0).then_inc(wbd_zero, 1)
        V.memset(VRS, 0.0)
        V.memset(FT[:, :, :, D:D + 1], 1.0)
        V.memset(FT[:, :, :, D + 1:], 0.0)
        V.drain()
        dve.wait_ge(e_ready, 4)
        dve.wait_ge(tr_emptied, 3 * NT)

        def final(i, g):
            j, half = g // 2, g % 2
            h = i * 2 + j
            t0 = 5 * half
            y = NUM[:, g % 2]
            dve.wait_ge(num_ready, i * 4 + g + 1)
            V.tensor_scalar(RD, y[:, :, D:D + 1], TINY, None, ALU.max)
            V.drain()
            V.reciprocal(RD, RD)
            V.drain()
            V.tensor_tensor(y[:, :, 0:D], y[:, :, 0:D], RD.to_broadcast([T, 5, D]), ALU.mult)
            V.drain()
            V.tensor_tensor(y[:, :, 0:D], y[:, :, 0:D],
                            RES[:, bass.ds(i % 2, 1), t0:t0 + 5, j * D:(j + 1) * D].rearrange("p a t c -> p (a t) c"), ALU.add)
            V.drain()
            xs = X[:, t0:t0 + 5, bass.ds(h * D, D)]
            V.scalar_tensor_tensor(out=xs, in0=y[:, :, 0:D], scalar=0.0, in1=xs, op0=ALU.max, op1=ALU.add).then_inc(num_used, 1)

        def pair(i):
            first = isinstance(i, int)
            if not first:
                dve.wait_ge(a2_filled, i * 6)
            for j in range(2):
                V.tensor_scalar(VRS[j * D:(j + 1) * D, j, :], ones[j * D:(j + 1) * D, 0:T],
                                vvn[j * D:(j + 1) * D, bass.ds(i * 2 + j + H, 1)], None, ALU.mult).then_inc(vrs_ready, 1)
            dve.wait_ge(g56_emptied, i * 15 + 5)
            for j in range(2):
                h = i * 2 + j
                for f in range(2):
                    V.tensor_tensor(F[:, :, f * DW:(f + 1) * DW], FT[:, :, j, :],
                                    EX[:, f, :, bass.ds(h, 1)].to_broadcast([T, NT, DW]), ALU.mult)
                V.drain().then_inc(f_ready, 1)
                dve.wait_ge(pf_hi, i * 2 + j + 1)
                V.tensor_tensor(PF[:, j, :, 1, :], F, PF[:, j, :, 0, :].bitcast(F32), ALU.subtract)
                V.drain().then_inc(pf_ready, 1)
            for g in range(4):
                j, half = g // 2, g % 2
                h = i * 2 + j
                dve.wait_ge(a2_emptied, i * 6 + 3 * j + 3)
                for s in range(NT):
                    n = g * 10 + s - BSLOTS
                    gg, ss = n // 10, n % 10
                    if not first or n >= 0:
                        if ss == 9:
                            dve.wait_ge(accb_filled, i * 20 + 5 * (gg + 1))
                        else:
                            dve.wait_ge(b1_used, i * 36 + 9 * gg + ss + 1)
                    V.scalar_tensor_tensor(out=B1[:, (g * 10 + s) % BSLOTS, :], in0=A2B[:, j, half * RH:(half + 1) * RH],
                                           scalar=GT[:, s, bass.ds(h, 1)], in1=AT[:, s, half * RH:(half + 1) * RH].bitcast(F32),
                                           op0=ALU.is_le, op1=ALU.mult).then_inc(b1_ready, 1)
                if g:
                    final(i, g - 1)
                elif not first:
                    final(i - 1, 3)

        pair(0)
        with nc.vector.Fori(1, NP) as i:
            pair(i)
        final(NP - 1, 3)
        V.drain().then_inc(stage_done, 1)
        if STOP <= 1:
            V.drain().then_inc(done, 1)
            return

        def route(L, k, normalised):
            ps = full(J.at[f"route{L}"])
            g = lambda n: RS[:, n]
            r = lambda n: R1[:, n, :]
            spread = lambda n: R1[:, n, :].unsqueeze(2).to_broadcast([T, NT, NE])
            prefb = pref.unsqueeze(1).to_broadcast([T, NT, NE])

            def step(ins):
                V.drain()

            step(V.tensor_tensor(g(0), ps[0:T, 0:NT * NE].rearrange("p (t e) -> p t e", e=NE),
                                 RB.unsqueeze(1).to_broadcast([T, NT, NE]), ALU.add).then_inc(dve_emptied, 1))
            step(V.tensor_reduce(r(0), g(0), AX.X, ALU.max))
            step(V.tensor_tensor(g(0), g(0), spread(0), ALU.subtract))
            V.drain().then_inc(gexp_in, 1)
            dve.wait_ge(gexp_out, k)
            step(V.tensor_reduce(r(1), g(1), AX.X, ALU.add))
            step(V.reciprocal(r(2), r(1)))
            step(V.tensor_tensor(g(2), g(1), spread(2), ALU.mult))
            src_p = 2
            for n in range(2):
                step(V.tensor_reduce(r(3 + n), g(src_p), AX.X, ALU.max))
                step(V.tensor_tensor(g(3), g(src_p), spread(3 + n), ALU.is_equal))
                step(V.tensor_tensor(g(4), g(3), prefb, ALU.mult))
                step(V.tensor_reduce(r(5), g(4), AX.X, ALU.max))
                step(V.tensor_tensor(g(5), prefb, spread(5), ALU.is_equal))
                if n == 0:
                    step(V.tensor_tensor(g(6), g(5), g(2), ALU.mult))
                    step(V.scalar_tensor_tensor(out=g(7), in0=g(5), scalar=-2.0, in1=g(2), op0=ALU.mult, op1=ALU.add))
                    src_p = 7
                else:
                    step(V.tensor_tensor(g(8), g(5), g(2), ALU.mult))
            step(V.tensor_tensor(GA, g(6), g(8), ALU.add))
            if normalised:
                step(V.tensor_tensor(r(6), r(3), r(4), ALU.add))
                step(V.tensor_scalar(r(6), r(6), 1e-9, None, ALU.add))
                step(V.reciprocal(r(7), r(6)))
                step(V.tensor_tensor(GA, GA, spread(7), ALU.mult))
            V.drain().then_inc(gates_ready, 1)
            add_rows(f"ebias{L}")

        layer_norm(1)
        dve.wait_ge(small_in, 48)
        route(1, 1, True)
        V.drain()
        f0 = J.filled(J.at["experts1"] - 1)
        with nc.vector.Fori(0, NE // 2) as i:
            for e in range(2):
                for t in range(NT):
                    for b in range(2):
                        n = 20 * e + 2 * t + b
                        dve.wait_ge(pe_filled, i * 40 + f0 + n + 1)
                        xs = X[:, t, b * HC:(b + 1) * HC]
                        V.scalar_tensor_tensor(out=xs, in0=bank(n)[0:T, 0:HC], scalar=GA[:, t, bass.ds(i * 2 + e, 1)],
                                               in1=xs, op0=ALU.mult, op1=ALU.add).then_inc(dve_emptied, 1)
                V.drain()
        V.drain().then_inc(stage_done, 1)
        if STOP <= 3:
            V.drain().then_inc(done, 1)
            return

        layer_norm(2)
        for r in range(18):
            q, c = r // 3, r % 3
            o, n = CH[c]
            dve.wait_ge(act_emptied, J.emptied("act", J.at["k1"] + r))
            V.tensor_tensor(QK[:, q, o:o + n], QK[:, q, o:o + n], K2[:, r % 2, 0:n], ALU.mult).then_inc(k2_used, 1)
        V.tensor_reduce(S4, SQ, AX.X, ALU.add)
        V.drain()
        V.drain().then_inc(norm_in, 1)
        dve.wait_ge(norm_out, 1)
        V.tensor_tensor(SC[:, 2], SC[:, 0], SC[:, 1], ALU.mult)
        V.tensor_tensor(SC[:, 3], S4[:, 0], S4[:, 1], ALU.mult)
        V.drain()
        V.scalar_tensor_tensor(out=SC[:, 4], in0=SC[:, 2], scalar=float(N), in1=SC[:, 3], op0=ALU.mult, op1=ALU.add)
        V.drain()
        V.tensor_tensor(SC[:, 4], SC[:, 4], SC[:, 1], ALU.mult)
        V.drain()
        V.reciprocal(SC[:, 5], SC[:, 4])
        V.drain()
        for r in range(18):
            q, c = r // 3, r % 3
            o, n = CH[c]
            ps = full(J.at["v1"] + r)
            V.scalar_tensor_tensor(out=QK[:, q, o:o + n], in0=ps[:, 0:n], scalar=SC[:, 5, q:q + 1], in1=QK[:, q, o:o + n],
                                   op0=ALU.mult, op1=ALU.mult).then_inc(dve_emptied, 1)

        V.drain()
        dve.wait_ge(mix_bias, 48)
        for b in range(2):
            V.tensor_tensor(X, X, BB1[:, b, :].unsqueeze(1).to_broadcast([T, NT, C]), ALU.add)
            V.drain()
        add_rows("proj1")
        for t in range(NT):
            d = AT[:, t, t * T:(t + 1) * T]
            V.tensor_tensor(d, d.bitcast(F32), ident[0:T, 0:T], ALU.add)
        V.drain().then_inc(loops, 1)
        V.drain().then_inc(stage_done, 1)
        for c, (o, n) in enumerate(CH):
            ps = full(J.at["deg"] + c)
            V.tensor_copy(DB[:, o:o + n], ps[:, 0:n]).then_inc(dve_emptied, 1)
        V.drain().then_inc(deg_sum, 1)
        dve.wait_ge(deg_root, 1)
        V.reciprocal(DB, DB).then_inc(deg_root, 1)
        for q in range(3):
            ps = full(J.at["dinv"] + q)
            w = min(4 * q + 4, NT) - 4 * q
            V.tensor_copy(DT[:, 4 * q:4 * q + w].unsqueeze(2), ps[0:T, 0:w * P].rearrange("p (t n) -> p t n", t=w)[:, :, 0:1]).then_inc(dve_emptied, 1)

        def low_parts(k):
            for r in range(20):
                t, b = r // 2, r % 2
                dve.wait_ge(hf_hi, 20 * k + r + 1)
                V.tensor_tensor(HH[:, 1, t, b * HC:(b + 1) * HC], HF[:, b, :],
                                HH[:, 0, t, b * HC:(b + 1) * HC].bitcast(F32), ALU.subtract).then_inc(hf_used, 1)

        low_parts(0)
        for r in range(18):
            o, n = CH[r % 3]
            ps = full(J.at["agg1"] + r)
            if r >= 2:
                dve.wait_ge(h1_ready, r - 1)
            V.tensor_tensor(TA[:, r % 2, 0:n], ps[:, 0:n], DB[:, o:o + n], ALU.mult).then_inc(dve_emptied, 1)
        low_parts(1)
        for r in range(20):
            t, b = r // 2, r % 2
            ps = full(J.at["agg2"] + r)
            xs = X[:, t, b * HC:(b + 1) * HC]
            V.scalar_tensor_tensor(out=xs, in0=ps[0:T, 0:HC], scalar=DT[:, t:t + 1], in1=xs, op0=ALU.mult,
                                   op1=ALU.add).then_inc(dve_emptied, 1)
        V.drain().then_inc(stage_done, 1)
        if STOP <= 4:
            V.drain().then_inc(done, 1)
            return

        layer_norm(3)
        dve.wait_ge(small_in, 48 + 64)
        route(3, 2, False)
        V.drain()
        f3 = J.filled(J.at["experts3"] - 1)
        with nc.vector.Fori(0, NE // 2) as i:
            for e in range(2):
                for r in range(20):
                    t, b = r // 2, r % 2
                    dve.wait_ge(pe_filled, i * 58 + f3 + 29 * e + 9 + r + 1)
                    xs = X[:, t, b * HC:(b + 1) * HC]
                    V.scalar_tensor_tensor(out=xs, in0=bank(9 + r)[0:T, 0:HC], scalar=GA[:, t, bass.ds(i * 2 + e, 1)],
                                           in1=xs, op0=ALU.mult, op1=ALU.add).then_inc(dve_emptied, 1)
                V.drain()
        V.drain().then_inc(done, 1)

    block_ctx.__exit__(None, None, None)


def kernel(x, src, dst, L0_gnn_W, L0_gnn_attn_l, L0_gnn_attn_r, L0_gnn_W_res, L0_mix_w_qkv, L0_mix_w_proj,
           L0_mix_b_proj, L0_ffn_router_w, L0_ffn_router_b, L0_ffn_expert_w, L0_ffn_expert_b, L1_gnn_W1, L1_gnn_b1,
           L1_gnn_W2, L1_gnn_b2, L1_mix_w_qkv, L1_mix_w_proj, L1_mix_b_proj, L1_ffn_Wg, L1_ffn_bg, L1_ffn_W1,
           L1_ffn_b1, L1_ffn_W2, L1_ffn_b2):
    import numpy as _np
    import concourse.bacc as _bacc
    from concourse.bass_utils import run_bass_kernel_spmd as _run

    g = _np.asarray
    attn = _np.concatenate([g(L0_gnn_attn_l)[0], g(L0_gnn_attn_r)[0]], axis=0).T
    given = [("x", g(x)), ("src", g(src)), ("dst", g(dst)), ("gW", g(L0_gnn_W)), ("gWT", g(L0_gnn_W).T),
             ("gWresT", g(L0_gnn_W_res).T), ("attnT", attn), ("w0", g(L0_mix_w_qkv)), ("wp0", g(L0_mix_w_proj)),
             ("bp0", g(L0_mix_b_proj)), ("rwT", g(L0_ffn_router_w).T), ("rb", g(L0_ffn_router_b)),
             ("ewT", g(L0_ffn_expert_w).transpose(0, 2, 1)), ("eb", g(L0_ffn_expert_b)), ("W1", g(L1_gnn_W1)),
             ("b1c", g(L1_gnn_b1).reshape(KC, P).T), ("W2", g(L1_gnn_W2)), ("b2", g(L1_gnn_b2)), ("w1", g(L1_mix_w_qkv)),
             ("wp1", g(L1_mix_w_proj)), ("bp1", g(L1_mix_b_proj)), ("fgT", g(L1_ffn_Wg).T), ("fbg", g(L1_ffn_bg)),
             ("fW1", g(L1_ffn_W1)), ("fb1c", g(L1_ffn_b1).reshape(NE, FH // P, P).transpose(2, 0, 1)), ("fW2", g(L1_ffn_W2)), ("fb2", g(L1_ffn_b2))]
    nc = _bacc.Bacc("TRN2", target_bir_lowering=False, num_devices=1)
    arrays, args = {}, {}
    for name, a in given:
        a = _np.ascontiguousarray(a)
        arrays[f"in_{name}"] = a
        args[name] = nc.dram_tensor(f"in_{name}", a.shape, mybir.dt.from_np(a.dtype), kind="ExternalInput").ap()
    out = nc.dram_tensor("out_x", (N, C), F32, kind="ExternalOutput").ap()
    graph_transformer(nc, out=out, **args)
    r = _run(nc, [arrays], core_ids=[0])
    return r.results[0]["out_x"]
```

```python
import concourse.bass as bass
from concourse import mybir

F32 = mybir.dt.float32
FR = mybir.dt.float32r
BF16 = mybir.dt.bfloat16
F16 = mybir.dt.float16
I32 = mybir.dt.int32
U32 = mybir.dt.uint32
ALU = mybir.AluOpType
ACT = mybir.ActivationFunctionType
AX = mybir.AxisListType

P = 128
N = 1250
NT, T = 10, 125
C = 768
KC = C // P
E = 20000
ET = E // T
H, D = 12, 64
NP = H // 2
DW = D + 2
NE = 8
FH = 384
KT = NT * 2
ET_MAX = (2 * N + NE * (P - 1)) // P
ET_MAX += ET_MAX % 2
ETC = ET_MAX + 2
CH = [(0, 418), (418, 416), (834, 416)]
XNB = 3
HC = C // 2
LN_EPS = 1e-5
SLOPE = 0.2
TINY = 1e-37
SLOTS = 4
BSLOTS = 4
RH = N // 2
STOP = 99


class Jobs:

    def __init__(self):
        self.owner, self.at = [], {}

    def add(self, name, owners):
        self.at[name] = len(self.owner)
        self.owner += owners

    def filled(self, m):
        return sum(o is not None for o in self.owner[:m + 1])

    def emptied(self, who, m):
        return sum(o == who for o in self.owner[:m + 1])


def plan_jobs():
    j = Jobs()
    a, v = "act", "dve"
    j.add("edges", [v])
    j.add("lnt0", [a] * 20)
    j.add("kv", [v, v, a, a] * NT)
    j.add("kvsum", [v] * NP)
    j.add("q0", [v] * 18)
    j.add("lin", [v] * 36)
    j.add("proj0", [v] * 20)
    j.add("attn_vec", [v])
    j.add("node_att", [v])
    j.add("att_rows", [v] * 3)
    j.add("att_max", [v])
    for L in (1, 2, 3):
        j.add(f"lnt{L}", [a] * 20)
        if L in (1, 3):
            j.add(f"route{L}", [v])
            j.add(f"rank{L}", [v])
            j.add(f"tokens{L}", [v])
            j.add(f"gatesT{L}", [a] * 3)
            j.add(f"ebias{L}", [v] * 20)
        else:
            j.add("q1", [a] * 18)
            j.add("k1", [a] * 18)
            j.add("v1", [v] * 18)
            j.add("proj1", [v] * 20)
            j.add("deg", [v] * 3)
            j.add("dinv", [v] * 3)
            j.add("conv1", [a] * 20)
            j.add("agg1", [v] * 18)
            j.add("conv2", [a] * 20)
            j.add("agg2", [v] * 20)
    return j


def graph_transformer(nc, xn_d, y_d, x, src, dst, gW, gWT, gWresT, attnT, w0, wp0, bp0, rwT, rb, ewT, eb,
                      W1, b1c, W2, b2, w1, wp1, bp1, fgT, fbg, fW1, fb1, fW2, fb2, out):
    J = plan_jobs()

    cursor = [(nc.sbuf_base + 63) // 32 * 32]

    def sb(name, shape, dt=F32):
        n = 1
        for s in shape[1:]:
            n *= s
        n *= 2 if dt in (BF16, F16) else 4
        t = nc.alloc_sbuf_tensor_at(name, shape, dt, offset=cursor[0])
        cursor[0] += (n + 31) // 32 * 32
        return t[:]

    PS = nc.alloc_psum_tensor("PS", [P, 8, 512], F32)[:]

    X = sb("X", [T, NT, C])
    xt_base = cursor[0]
    XT = sb("XT", [P, KC, N])
    at_base = cursor[0]
    AT = sb("AT", [T, NT, N], FR)
    ident = sb("ident", [P, P])
    ones = sb("ones", [P, P])
    onesr = sb("onesr", [P, P], FR)
    stats = sb("stats", [T, NT, 12])
    mv = sb("mv", [T, NT, 2])
    std = sb("std", [T, NT])
    rstd = sb("rstd", [T, NT])
    GT = sb("GT", [T, NT, 2 * H])
    GB = sb("GB", [T, H])
    EX = sb("EX", [T, 4, NT, H])
    vvn = sb("vvn", [P, 2 * H])
    pref = sb("pref", [T, NE])
    pcol = sb("pcol", [P, 1])
    k128 = sb("k128", [T, 32])
    tq = sb("tq", [T, NT])
    io128 = sb("io128", [T, P], BF16)
    before = sb("before", [T, T])
    base = cursor[0]
    top = nc.sbuf_usable_end // 32 * 32
    cursor[0] = top - XNB * C * 4
    XN = sb("XN", [T, XNB, C])
    cursor[0] = top - XNB * C * 4
    pref_i = sb("pref_i", [T, NE], I32)
    pcol_i = sb("pcol_i", [P, 1], I32)
    k128_i = sb("k128_i", [T, 32], I32)
    tq_i = sb("tq_i", [T, NT], I32)
    io128_i = sb("io128_i", [T, P], I32)
    cursor[0] = top - XNB * C * 4 - 8192
    EI = sb("EI", [80, 4, T], I32)
    EF = sb("EF", [80, 4, T])
    ES = sb("ES", [T, 2, ET])
    wide = sb("wide", [D, P])
    attn_sb = sb("attn_sb", [D, 2 * H])
    vv = sb("vv", [P, 2 * H])
    vz = sb("vz", [P, NP, 2 * H])
    assert cursor[0] <= top - XNB * C * 4

    cursor[0] = base
    WS = sb("WS", [P, 2, KC * C])
    small = cursor[0]
    VR = sb("VR", [T, NT, NP, P + 2])
    KVB = sb("KVB", [P, NP, P])
    KSB = sb("KSB", [P, NP, P])
    TK = sb("TK", [T, 2, HC])
    assert cursor[0] <= top - XNB * C * 4 - 8192, cursor[0]
    cursor[0] = small
    QT = sb("QT", [P, KC, N])
    cursor[0] = at_base
    KR = sb("KR", [T, NT, C])
    TQ = sb("TQ", [P, 2, 2, 418])
    BB = sb("BB", [T, C])
    assert cursor[0] <= at_base + NT * N * 4

    cursor[0] = base
    ZZ = sb("ZZ", [T, 4, NT, H])
    iota = sb("iota", [P, N], F16)
    iota_i = sb("iota_i", [P, N], I32)
    OHS = sb("OHS", [T, SLOTS, N], BF16)
    OHD = sb("OHD", [T, SLOTS, T], BF16)
    zeros = sb("zeros", [T, 512], BF16)
    AROW = sb("AROW", [T, 2, N])
    gidx = sb("gidx", [80, 2, NT])
    gidx_i = sb("gidx_i", [80, 2, NT], I32)
    tidx = sb("tidx", [80, 2])
    tidx_i = sb("tidx_i", [80, 2], I32)
    mnx = sb("mnx", [80, 2, 2])
    hit = sb("hit", [80, 2, 2, NT])
    rng = sb("rng", [2 * NT, 1])
    span = sb("span", [1, 8, NT])
    table = sb("table", [1, 3, NT], I32)
    turns = sb("turns", [1, NT, ET // SLOTS])
    gmax = sb("gmax", [H, 4])
    gdiag = sb("gdiag", [H, H])
    assert cursor[0] <= top - XNB * C * 4 - 8192

    cursor[0] = base
    PF = sb("PF", [T, 2, NT, 2, 2 * DW], FR)
    B1 = sb("B1", [T, BSLOTS, RH], FR)
    XPS = sb("XPS", [P, N])
    VRS = sb("VRS", [P, 2, T])
    WBD = sb("WBD", [P, 2 * P])
    FT = sb("FT", [T, NT, 2, DW])
    RES = sb("RES", [T, 2, NT, P])
    F = sb("F", [T, NT, 2 * DW])
    A2B = sb("A2B", [T, 2, N])
    Y1 = sb("Y1", [T, 2, 5, 4 * DW])
    YA = sb("YA", [T, NT, 2, 2, DW])
    YT = sb("YT", [T, 5, 2 * DW])
    NUM = sb("NUM", [T, 2, 5, DW])
    RD = sb("RD", [T, 5, 1])

    cursor[0] = small
    RW = sb("RW", [P, KC, NE])
    RB = sb("RB", [T, NE])
    EB = sb("EB", [NE, C])
    GA = sb("GA", [T, NT, NE])
    RS = sb("RS", [T, 10, NT, NE])
    R1 = sb("R1", [T, 8, NT])
    WT = sb("WT", [NE, N])
    SEL = sb("SEL", [T, NT, NE])
    SELB = sb("SELB", [T, NT + 1, NE])
    CNT = sb("CNT", [T, NE])
    CG = sb("CG", [T, NE, NT])
    EB4 = sb("EB4", [T, 4, NE])
    POS = sb("POS", [T, NT, 2])
    GE = sb("GE", [T, KT, ETC + 1])
    TL = sb("TL", [T, KT])
    OHR = sb("OHR", [T, KT, P], BF16)
    OT = sb("OT", [T, KT, ETC])
    TV = sb("TV", [T, KT, 2, ETC], BF16)
    TOKF = sb("TOKF", [P, ETC])
    TOK = sb("TOK", [P, ETC])
    XE = sb("XE", [1, ETC, NE])
    XT1 = sb("XT1", [1, 4, ETC])
    TAB = sb("TAB", [1, 3, ETC], I32)
    IDXF = sb("IDXF", [P, 2])
    IDX = sb("IDX", [P, 2], U32)
    assert cursor[0] <= top - XNB * C * 4
    cursor[0] = xt_base
    XG = sb("XG", [P, 2, C])
    XGT = sb("XGT", [P, 2, KC, P])
    YS = sb("YS", [P, 2, C])
    YG = sb("YG", [T, 2, C])
    assert cursor[0] <= at_base
    cursor[0] = at_base
    BH = sb("BH", [P, NE, FH])
    HR = sb("HR", [P, 2, FH])
    HT = sb("HT", [P, FH // P, P])
    assert cursor[0] <= at_base + NT * N * 4
    cursor[0] = small
    QK = sb("QK", [P, KC, N])
    K2 = sb("K2", [P, 2, 418])
    JK = sb("JK", [P, 2, 418])
    SQ = sb("SQ", [P, 4, KC, 3])
    S4 = sb("S4", [P, 4, KC])
    SC = sb("SC", [P, 6, KC])
    BB1 = sb("BB1", [T, 2, C])
    assert cursor[0] <= top - XNB * C * 4
    cursor[0] = base + KC * C * 4
    HH = sb("HH", [T, 2, NT, C], FR)
    HF = sb("HF", [T, 2, HC])
    DB = sb("DB", [P, N])
    DT = sb("DT", [T, NT])
    TA = sb("TA", [P, 2, 418])
    B1C = sb("B1C", [P, KC])

    sem = nc.alloc_semaphore
    x_in, e_in, gw_in, c_in = sem("x_in"), sem("e_in"), sem("gw_in"), sem("c_in")
    w_in = [sem("w_in0"), sem("w_in1")]
    consts = sem("consts")
    pe_filled, act_emptied, dve_emptied = sem("pe_filled"), sem("act_emptied"), sem("dve_emptied")
    ln_var, ln_std, xn_ready = sem("ln_var"), sem("ln_std"), sem("xn_ready")
    wide_ready, edge_f, ranged, table_ready = sem("wide_ready"), sem("edge_f"), sem("ranged"), sem("table_ready")
    oh_ready, oh_free, acc_done, arow_ready, tr_filled, tr_emptied = (sem(s) for s in (
        "oh_ready", "oh_free", "acc_done", "arow_ready", "tr_filled", "tr_emptied"))
    vz_ready, gdiag_ready, z_ready, e_ready = sem("vz_ready"), sem("gdiag_ready"), sem("z_ready"), sem("e_ready")
    wbd_ready, wbd_zero, vrs_ready = sem("wbd_ready"), sem("wbd_zero"), sem("vrs_ready")
    xp_staged, xp_used, g56_filled, g56_emptied = (sem(s) for s in ("xp_staged", "xp_used", "g56_filled", "g56_emptied"))
    a2_filled, a2_emptied = sem("a2_filled"), sem("a2_emptied")
    f_ready, pf_hi, pf_ready = sem("f_ready"), sem("pf_hi"), sem("pf_ready")
    b1_ready, b1_used, accb_filled, y_emptied, y_used, pool_step, num_ready, num_used = (sem(s) for s in (
        "b1_ready", "b1_used", "accb_filled", "y_emptied", "y_used", "pool_step", "num_ready", "num_used"))
    kexp, qexp, kvb_zero = sem("kexp"), sem("qexp"), sem("kvb_zero")
    gexp_in, gexp_out, gates_ready = sem("gexp_in"), sem("gexp_out"), sem("gates_ready")
    w_used, sum_step = sem("w_used"), sem("sum_step")
    k2_ready, k2_used, deg_sum, deg_root, hf_hi, hf_used, h1_ready, loops = (sem(s) for s in (
        "k2_ready", "k2_used", "deg_sum", "deg_root", "hf_hi", "hf_used", "h1_ready", "loops"))
    norm_in, norm_out = sem("norm_in"), sem("norm_out")
    mix_bias, small_in, done, stored = sem("mix_bias"), sem("small_in"), sem("done"), sem("stored")
    misc_in = sem("misc_in")
    y_cleared = sem("y_cleared")
    stage_done = sem("stage_done")
    xn_out = [sem(f"xn_out{b}") for b in range(XNB)]
    sel_ready, ranked, tab_ready, y_all = sem("sel_ready"), sem("ranked"), sem("tab_ready"), sem("y_all")
    xg_in, turned_n, xgt_ready, y_filled, y_free, ys_out, yg_in, yg_used, hid_filled, hid_summed, hid_ready, ht_filled, \
        ht_ready = ({L: [sem(f"{n}{L}{b}") for b in range(2)] for L in (1, 3)} for n in (
            "xg_in", "turned_n", "xgt_ready", "y_filled", "y_free", "ys_out", "yg_in", "yg_used", "hid_filled",
            "hid_summed", "hid_ready", "ht_filled", "ht_ready"))
    turned_n, xgt_ready, y_filled, y_free, yg_used, hid_filled, hid_summed, hid_ready, ht_filled, ht_ready = (
        {L: d[L][0] for L in d} for d in (turned_n, xgt_ready, y_filled, y_free, yg_used, hid_filled, hid_summed,
                                          hid_ready, ht_filled, ht_ready))

    W3 = [WS[:, s, :].rearrange("p (k c) -> p k c", k=KC) for s in range(2)]

    def bank(m):
        return PS[:, m % 8, :]

    def xn_stores(L, b):
        return 16 * (len(range(b, NT, XNB)) * (1 if L == 1 else 2))

    block_ctx = nc.Block()
    block = block_ctx.__enter__()

    units = [("w0", 1), ("w0", 2), ("w0", 0), ("wp0", 0)] + [("ew", e) for e in range(NE)] \
        + [("w1", 0), ("w1", 1), ("w1", 2), ("wp1", 0), ("W1", 0), ("W2", 0)] + [("ff", e) for e in range(NE)]
    U_EW, U_MIX1, U_GCN, U_FF = 4, 12, 16, 18
    slot_of = [u % 2 if u < U_GCN or u >= U_FF else 0 for u in range(len(units))]
    copies = [2 if kind == "ff" else 1 for kind, e in units]

    def arrived(u):
        return 16 * sum(copies[v] for v in range(u + 1) if slot_of[v] == slot_of[u])

    last = lambda name, n: J.at[name] + n - 1
    used = [last("kv", 40), last("kv", 40), last("q0", 18), last("proj0", 20)] \
        + [None] * NE \
        + [last("q1", 18), last("k1", 18), last("v1", 18), last("proj1", 20), last("conv1", 20), last("conv2", 20)]

    @block.sync
    def _(sp):
        sp.dma_start(X, x.rearrange("(t p) c -> p t c", p=T)).then_inc(x_in, 16)
        sp.dma_start(EI[:, 0:2, :], src.rearrange("(a p e) -> p a e", a=2, p=80)).then_inc(e_in, 16)
        sp.dma_start(EI[:, 2:4, :], dst.rearrange("(a p e) -> p a e", a=2, p=80)).then_inc(e_in, 16)

        def load(u):
            kind, e = units[u]
            s = slot_of[u]
            if kind in ("w0", "w1"):
                w = (w0 if kind == "w0" else w1).rearrange("(k p) n -> p k n", p=P)
                sp.dma_start(W3[s], w[:, :, e * C:(e + 1) * C]).then_inc(w_in[s], 16)
            elif kind == "ff":
                sp.dma_start(WS[:, s, 0:KC * FH].rearrange("p (k h) -> p k h", k=KC),
                             fW1[e].rearrange("(k p) h -> p k h", p=P)).then_inc(w_in[s], 16)
                sp.dma_start(WS[:, s, KC * FH:].rearrange("p (k h) -> p k h", k=FH // P),
                             fW2[e].rearrange("(k p) h -> p k h", p=P)).then_inc(w_in[s], 16)
            else:
                w = {"wp0": wp0, "wp1": wp1, "W1": W1, "W2": W2}.get(kind)
                w = ewT[e] if w is None else w
                sp.dma_start(W3[s], w.rearrange("(k p) n -> p k n", p=P)).then_inc(w_in[s], 16)

        def unit_left(u):
            sp.wait_ge(pe_filled, J.filled(used[u]))

        def expert_loads(L, u0, u1):
            sp.wait_ge(tab_ready, 1 if L == 1 else 2)
            for e in range(2, NE + (u1 > u0 + NE) * 0):
                first = nc.sync.value_load(TAB[0:1, 1, e - 1:e], min_val=0, max_val=ET_MAX)
                sp.wait_ge(y_filled[L], first + 1)
                load(u0 + e)
            for e in range(2):
                pass

        load(0)
        load(1)
        spare = 2 * N // P * P
        sp.dma_start(y_d[spare:, :], x[0:ET_MAX * P - spare, :]).then_inc(y_cleared, 16)
        sp.dma_start(wide[:, 0:D], gW).then_inc(gw_in, 16)
        sp.dma_start(wide[:, D:P], gW).then_inc(gw_in, 16)
        sp.dma_start(attn_sb, attnT).then_inc(gw_in, 16)
        sp.dma_start(BB, bp0.partition_broadcast(T)).then_inc(mix_bias, 16)
        for u in (2, 3):
            unit_left(u - 2)
            load(u)
        sp.wait_ge(wbd_zero, 1)
        for o in (0, D):
            sp.dma_start(WBD[o:o + D, o:o + D], gWT).then_inc(wbd_ready, 16)
            sp.dma_start(WBD[o:o + D, P + o:P + o + D], gWresT).then_inc(wbd_ready, 16)
        if STOP <= 1:
            sp.wait_ge(done, 1)
            sp.dma_start(out.rearrange("(t p) c -> p t c", p=T), X).then_inc(stored, 16)
            sp.wait_ge(stored, 16)
            return
        sp.wait_ge(stage_done, 1)
        load(U_EW)
        load(U_EW + 1)
        sp.dma_start(RW, rwT.rearrange("(k p) e -> p k e", p=P)).then_inc(small_in, 16)
        sp.dma_start(RB, rb.partition_broadcast(T)).then_inc(small_in, 16)
        sp.dma_start(EB, eb).then_inc(small_in, 16)
        expert_loads(1, U_EW, U_MIX1)
        if STOP > 3:
            sp.wait_ge(stage_done, 2)
            load(U_MIX1)
            load(U_MIX1 + 1)
            sp.dma_start(BB1[:, 0, :], b2.partition_broadcast(T)).then_inc(mix_bias, 16)
            sp.dma_start(BB1[:, 1, :], bp1.partition_broadcast(T)).then_inc(mix_bias, 16)
            for u in range(U_MIX1 + 2, U_GCN + 1):
                unit_left(u - 2)
                load(u)
            sp.wait_ge(stage_done, 3)
            sp.dma_start(B1C, b1c).then_inc(misc_in, 16)
            unit_left(U_GCN)
            load(U_GCN + 1)
        if STOP > 4:
            unit_left(U_GCN + 1)
            load(U_FF)
            sp.wait_ge(stage_done, 4)
            load(U_FF + 1)
            sp.dma_start(RW, fgT.rearrange("(k p) e -> p k e", p=P)).then_inc(small_in, 16)
            sp.dma_start(RB, fbg.partition_broadcast(T)).then_inc(small_in, 16)
            sp.dma_start(EB, fb2).then_inc(small_in, 16)
            sp.dma_start(BH, fb1.partition_broadcast(P)).then_inc(small_in, 16)
            expert_loads(3, U_FF, len(units))
        sp.wait_ge(done, 1)
        sp.dma_start(out.rearrange("(t p) c -> p t c", p=T), X).then_inc(stored, 16)
        sp.wait_ge(stored, 16)

    @block.gpsimd
    def _(pool):
        nc.gpsimd.memset(ident, 0.0).then_inc(pool_step, 1)
        pool.wait_ge(pool_step, 1)
        nc.gpsimd.affine_select(out=ident, in_=ident, compare_op=ALU.not_equal, fill=1.0, base=0,
                                pattern=[[-1, P]], channel_multiplier=1).then_inc(consts, 1)
        nc.gpsimd.iota(pref_i, pattern=[[-1, NE]], base=NE, channel_multiplier=0).then_inc(consts, 1)
        nc.gpsimd.iota(pcol_i, pattern=[[1, 1]], base=0, channel_multiplier=1).then_inc(consts, 1)
        nc.gpsimd.iota(k128_i, pattern=[[P, 32]], base=0, channel_multiplier=0).then_inc(consts, 1)
        nc.gpsimd.iota(tq_i, pattern=[[1, NT]], base=0, channel_multiplier=0).then_inc(consts, 1)
        nc.gpsimd.iota(io128_i, pattern=[[1, P]], base=0, channel_multiplier=0).then_inc(consts, 1)
        pool.wait_ge(pe_filled, J.filled(J.at["proj0"] + 19))
        nc.gpsimd.iota(iota_i, pattern=[[1, N]], base=0, channel_multiplier=0).then_inc(consts, 1)
        nc.gpsimd.iota(gidx_i, pattern=[[T, 2], [T, NT]], base=0, channel_multiplier=0).then_inc(consts, 1)
        nc.gpsimd.iota(tidx_i, pattern=[[80, 2]], base=0, channel_multiplier=1).then_inc(consts, 1)
        steps = [1]

        def combine(i, g):
            j, half = g // 2, g % 2
            h = i * 2 + j
            t0 = half * 5
            y = Y1[:, g % 2]
            n0 = 1 + 4 * (i * 4 + g)
            if g or not isinstance(i, int):
                pool.wait_ge(num_ready, i * 4 + g)
            pool.wait_ge(y_emptied, i * 20 + 5 * (g + 1))
            pool.wait_ge(g56_emptied, i * 15 + 15)
            if g >= 2 or not isinstance(i, int):
                pool.wait_ge(num_used, i * 4 + g - 1)
            z = NUM[:, g % 2]
            nc.gpsimd.tensor_tensor(YT, y[:, :, 0:2 * DW], y[:, :, 2 * DW:], ALU.add).then_inc(y_used, 1)
            nc.gpsimd.tensor_tensor(z, YA[:, t0:t0 + 5, j, 0, :], YA[:, t0:t0 + 5, j, 1, :], ALU.add).then_inc(pool_step, 1)
            pool.wait_ge(y_used, i * 4 + g + 1)
            pool.wait_ge(pool_step, n0 + 1)
            nc.gpsimd.tensor_tensor(z, z, YT[:, :, DW:], ALU.subtract).then_inc(pool_step, 1)
            q1 = EX[:, 2, t0:t0 + 5, bass.ds(h, 1)].to_broadcast([T, 5, DW])
            q2 = EX[:, 3, t0:t0 + 5, bass.ds(h, 1)].to_broadcast([T, 5, DW])
            pool.wait_ge(pool_step, n0 + 2)
            nc.gpsimd.tensor_tensor(z, z, q2, ALU.mult).then_inc(pool_step, 1)
            nc.gpsimd.tensor_tensor(YT[:, :, 0:DW], YT[:, :, 0:DW], q1, ALU.mult).then_inc(pool_step, 1)
            pool.wait_ge(pool_step, n0 + 4)
            nc.gpsimd.tensor_tensor(z, z, YT[:, :, 0:DW], ALU.add).then_inc(num_ready, 1)

        if STOP >= 1:
            pool.wait_ge(e_ready, 4)
            for g in range(4):
                combine(0, g)
            with nc.gpsimd.Fori(1, NP) as i:
                for g in range(4):
                    combine(i, g)

        def gather(L, n, b):
            tok = TOK[:, bass.ds(n, 1)]
            nc.gpsimd.tensor_tensor(IDXF[:, b:b + 1], tok, ones[:, 0:1], ALU.mult)
            pool.drain()
            nc.gpsimd.tensor_copy(IDX[:, b:b + 1], IDXF[:, b:b + 1])
            pool.drain()
            nc.gpsimd.indirect_dma_start(out=XG[:, b, :], out_offset=None, in_=xn_d,
                                         in_offset=bass.IndirectOffsetOnAxis(ap=IDX[:, b:b + 1], axis=0)
                                         ).then_inc(xg_in[L][b], 16)

        def gathers(L, k):
            ahead = 1 if L == 1 else 2
            pool.wait_ge(tab_ready, k)
            for b in range(XNB):
                pool.wait_ge(xn_out[b], xn_stores(L, b))
            n = nc.gpsimd.value_load(TAB[0:1, 2, 0:1], min_val=1, max_val=ET_MAX // 2)
            for a in range(ahead):
                gather(L, a, a)
            with nc.gpsimd.Fori(0, n) as i:
                for a in range(2):
                    b = (a + ahead) % 2
                    pool.wait_ge(turned_n[L], i * 2 + a + ahead)
                    gather(L, i * 2 + a + ahead, b)
            for b in range(2):
                pool.wait_ge(ys_out[L][b], n * 16 + 16)
            for q in range(KT):
                if q >= 2:
                    pool.wait_ge(yg_used[L], q - 1)
                idx = IDX[0:T, q % 2:q % 2 + 1]
                pos = POS[:, q // 2, q % 2:q % 2 + 1]
                nc.gpsimd.tensor_tensor(IDXF[0:T, q % 2:q % 2 + 1], pos, ones[0:T, 0:1], ALU.mult)
                pool.drain()
                nc.gpsimd.tensor_copy(idx, IDXF[0:T, q % 2:q % 2 + 1])
                pool.drain()
                nc.gpsimd.indirect_dma_start(out=YG[:, q % 2, :], out_offset=None, in_=y_d,
                                             in_offset=bass.IndirectOffsetOnAxis(ap=idx, axis=0)
                                             ).then_inc(yg_in[L][q % 2], 16)

        if STOP > 1:
            gathers(1, 1)
        if STOP > 4:
            gathers(3, 2)

    @block.tensor
    def _(pe):
        def begin(m):
            for k in range(m - 8, -1, -1):
                if k % 8 == m % 8 and J.owner[k]:
                    pe.wait_ge(act_emptied if J.owner[k] == "act" else dve_emptied, J.emptied(J.owner[k], k))
                    break
            return bank(m)

        def transposes(L):
            m0 = J.at[f"lnt{L}"]
            for t in range(NT):
                pe.wait_ge(xn_ready, L * NT + t + 1)
                for b in range(2):
                    ps = begin(m0 + 2 * t + b)
                    for k in range(3):
                        last = nc.tensor.transpose(ps[:, k * T:(k + 1) * T],
                                                   XN[:, t % XNB, (3 * b + k) * P:(3 * b + k + 1) * P], ident[0:T, 0:T])
                    last.then_inc(pe_filled, 1)

        def xt_ready(L):
            m = J.at[f"lnt{L}"] + 19
            pe.wait_ge(act_emptied, J.emptied("act", m))

        def weights(u):
            pe.wait_ge(w_in[slot_of[u]], arrived(u))
            return W3[slot_of[u]]

        def rows(m0, lhsT, w, t, halves=2, last_inc=None):
            for b in range(halves):
                ps = begin(m0 + b)
                for k in range(KC):
                    last = nc.tensor.matmul(ps[0:T, 0:HC], lhsT[:, k, t * T:(t + 1) * T], w[:, k, b * HC:(b + 1) * HC],
                                            start=(k == 0), stop=(k == KC - 1))
                last.then_inc(pe_filled, 1)

        def columns(m0, w, rhs):
            for q in range(KC):
                for c, (o, n) in enumerate(CH):
                    ps = begin(m0 + 3 * q + c)
                    for k in range(KC):
                        last = nc.tensor.matmul(ps[:, 0:n], w[:, k, q * P:(q + 1) * P], rhs[:, k, o:o + n],
                                                start=(k == 0), stop=(k == KC - 1))
                    last.then_inc(pe_filled, 1)

        pe.wait_ge(consts, 1)
        pe.wait_ge(edge_f, 1)
        ps = begin(0)
        for k in range(4):
            last = nc.tensor.transpose(ps[0:T, k * 80:(k + 1) * 80], EF[:, k, :], ident[0:80, 0:80])
        last.then_inc(pe_filled, 1)
        transposes(0)
        xt_ready(0)
        wk, wv = weights(0), weights(1)
        for t in range(NT):
            m = J.at["kv"] + 4 * t
            rows(m, XT, wk, t)
            rows(m + 2, XT, wv, t)
        pe.wait_ge(dve_emptied, J.emptied("dve", J.at["kvsum"] - 1))
        pe.wait_ge(act_emptied, J.emptied("act", J.at["kvsum"] - 1))
        for p in range(NP):
            ps = begin(J.at["kvsum"] + p)
            for t in range(NT):
                last = nc.tensor.matmul(ps[:, 0:P + 2], KR[:, t, p * P:(p + 1) * P], VR[:, t, p, :],
                                        start=(t == 0), stop=(t == NT - 1))
            last.then_inc(pe_filled, 1)
        columns(J.at["q0"], weights(2), XT)
        for p in range(NP):
            for c, (o, n) in enumerate(CH):
                m = J.at["lin"] + 6 * p + 2 * c
                pe.wait_ge(dve_emptied, J.emptied("dve", J.at["q0"] + 3 * p + c))
                nc.tensor.matmul(begin(m)[:, 0:n], KSB[:, p, :], QT[:, p, o:o + n], start=True, stop=True).then_inc(pe_filled, 1)
                nc.tensor.matmul(begin(m + 1)[:, 0:n], KVB[:, p, :], QT[:, p, o:o + n], start=True, stop=True).then_inc(pe_filled, 1)
        w = weights(3)
        pe.wait_ge(dve_emptied, J.emptied("dve", J.at["proj0"] - 1))
        for t in range(NT):
            rows(J.at["proj0"] + 2 * t, QT, w, t)
        pe.wait_ge(gw_in, 48)
        ps = begin(J.at["attn_vec"])
        nc.tensor.matmul(ps[:, 0:2 * H], wide, attn_sb, start=True, stop=True).then_inc(pe_filled, 1)
        xt_ready(0)
        pe.wait_ge(vz_ready, 1)
        ps = begin(J.at["node_att"])
        for t in range(NT):
            for k in range(KC):
                last = nc.tensor.matmul(ps[0:T, t * 2 * H:(t + 1) * 2 * H], XT[:, k, t * T:(t + 1) * T], vz[:, k, :],
                                        start=(k == 0), stop=(k == KC - 1))
        last.then_inc(pe_filled, 1)
        for c, (o, n) in enumerate(CH):
            ps = begin(J.at["att_rows"] + c)
            for k in range(KC):
                last = nc.tensor.matmul(ps[0:H, 0:n], vz[:, k, 0:H], XT[:, k, o:o + n], start=(k == 0), stop=(k == KC - 1))
            last.then_inc(pe_filled, 1)
        pe.wait_ge(gdiag_ready, 1)
        ps = begin(J.at["att_max"])
        nc.tensor.matmul(ps[0:T, 0:H], ones[0:H, 0:T], gdiag, start=True, stop=True).then_inc(pe_filled, 1)

        pe.wait_ge(ranged, 1)
        pe.wait_ge(dve_emptied, J.emptied("dve", J.at["att_max"]))
        ps = PS[:, 7, :]
        for a in range(2):
            last = nc.tensor.transpose(ps[0:2 * NT, a * 80:(a + 1) * 80], hit[:, a, :, :].rearrange("p a b -> p (a b)"),
                                       ident[0:80, 0:80])
        last.then_inc(tr_filled, 1)
        pe.wait_ge(ranged, 2)
        nc.tensor.transpose(ps[0:1, 256:256 + 2 * NT], rng, ident[0:2 * NT, 0:2 * NT]).then_inc(tr_filled, 1)
        pe.wait_ge(table_ready, 1)

        def spread(g):
            pe.wait_ge(arow_ready, 3 * (g + 1))
            for q in range(3):
                r = 3 * g + q
                if r >= 2:
                    pe.wait_ge(tr_emptied, r - 1)
                for k in range(4 * q, min(4 * q + 4, NT)):
                    last = nc.tensor.transpose(PS[0:T, 6 + r % 2, (k % 4) * T:(k % 4 + 1) * T],
                                               AROW[:, g % 2, k * T:(k + 1) * T], ident[0:T, 0:T])
                last.then_inc(tr_filled, 1)

        for g in range(NT):
            n = nc.tensor.value_load(table[0:1, 1, g:g + 1], min_val=1, max_val=ET // SLOTS)
            done_before = nc.tensor.value_load(table[0:1, 2, g:g + 1], min_val=0, max_val=ET * NT // SLOTS)
            if g >= 2:
                pe.wait_ge(arow_ready, 3 * (g - 1))
            for c, (o, w) in enumerate(CH):
                nc.tensor.matmul(PS[0:T, 3 * (g % 2) + c, 0:w], zeros[:, 0:T], zeros[:, 0:w], start=True, stop=True)
            with nc.tensor.Fori(0, n) as j:
                u = done_before + j
                for k in range(SLOTS):
                    pe.wait_ge(oh_ready, u * (2 * SLOTS) + 2 * k + 2)
                    for c, (o, w) in enumerate(CH):
                        last = nc.tensor.matmul(PS[0:T, 3 * (g % 2) + c, 0:w], OHD[:, k, :], OHS[:, k, o:o + w],
                                                start=False, stop=True, skip_group_check=True)
                    last.then_inc(oh_free, 1)
            nc.tensor.matmul(PS[0:T, 3 * (g % 2) + 2, 0:16], zeros[:, 0:T], zeros[:, 0:16], start=False, stop=True,
                             skip_group_check=True).then_inc(acc_done, 1)
            if g >= 1:
                spread(g - 1)
        spread(NT - 1)
        if STOP <= 0:
            return

        pe.wait_ge(wbd_ready, 64)
        pe.wait_ge(tr_emptied, 3 * NT)

        def pair(i):
            first = isinstance(i, int)
            pe.wait_ge(xp_staged, i + 1)
            for r in range(5):
                if r >= 2:
                    pe.wait_ge(g56_emptied, i * 15 + r - 1)
                else:
                    pe.wait_ge(g56_emptied, i * 15)
                for k in range(2):
                    last = nc.tensor.matmul(PS[0:T, 5 + r % 2, k * 256:(k + 1) * 256],
                                            XPS[:, (2 * r + k) * T:(2 * r + k + 1) * T], WBD, start=True, stop=True)
                last.then_inc(g56_filled, 1)
            pe.wait_ge(vrs_ready, i * 2 + 2)
            for j in range(2):
                for c, (o, n) in enumerate(CH):
                    r = 3 * j + c
                    if not first or r:
                        pe.wait_ge(a2_emptied, i * 6 + r)
                    last = nc.tensor.matmul(PS[0:T, 7, 0:n], VRS[:, j, :], XPS[:, o:o + n], start=True, stop=True)
                    last.then_inc(a2_filled, 1)
            pe.wait_ge(pf_ready, i * 2 + 2)
            for r in range(NT):
                pe.wait_ge(g56_emptied, i * 15 + 5 + r - 1)
                b = 5 + (r + 1) % 2
                for s in range(NT):
                    last = nc.tensor.matmul(PS[0:T, b, 0:4 * DW], AT[:, s, r * T:(r + 1) * T], PF[:, :, s, :, DW:],
                                            start=(s == 0), stop=(s == NT - 1))
                last.then_inc(g56_filled, 1)
            for g in range(4):
                j, half = g // 2, g % 2
                for s in range(NT):
                    pe.wait_ge(b1_ready, i * 40 + g * 10 + s + 1)
                    for b in range(5):
                        if s == 0 and (g or not first):
                            pe.wait_ge(y_emptied, i * 20 + 5 * (g - 1) + b + 1 if g else i * 20)
                        last = nc.tensor.matmul(PS[0:T, b, 0:4 * DW], B1[:, (g * 10 + s) % BSLOTS, b * T:(b + 1) * T],
                                                PF[:, j, s, :, :].rearrange("p a b -> p (a b)"),
                                                start=(s == 0), stop=(s == NT - 1))
                        if s == NT - 1 and b < 4:
                            last.then_inc(accb_filled, 1)
                    if s == NT - 1:
                        last.then_inc(accb_filled, 1)
                    else:
                        last.then_inc(b1_used, 1)

        pair(0)
        with nc.tensor.Fori(1, NP) as i:
            pair(i)
        if STOP <= 1:
            return
        pe.wait_ge(y_emptied, 20 * NP)
        pe.wait_ge(g56_emptied, 15 * NP)
        pe.wait_ge(a2_emptied, 6 * NP)

        def route(L):
            xt_ready(L)
            pe.wait_ge(small_in, 48 if L == 1 else 48 + 64)
            ps = begin(J.at[f"route{L}"])
            for t in range(NT):
                for k in range(KC):
                    last = nc.tensor.matmul(ps[0:T, t * NE:(t + 1) * NE], XT[:, k, t * T:(t + 1) * T], RW[:, k, :],
                                            start=(k == 0), stop=(k == KC - 1))
            last.then_inc(pe_filled, 1)
            k = 1 if L == 1 else 2
            pe.wait_ge(sel_ready, k)
            ps = begin(J.at[f"rank{L}"])
            n = NT * NE
            nc.tensor.matmul(ps[0:T, 0:n], before, SEL.rearrange("p t e -> p (t e)"), start=True, stop=False)
            nc.tensor.matmul(ps[0:T, 0:n], ones[0:T, 0:T], SELB[:, 0:NT, :].rearrange("p t e -> p (t e)"), start=False, stop=True)
            nc.tensor.matmul(ps[0:T, n:n + NE], ones[0:T, 0:T], SELB[:, NT, :], start=True, stop=True).then_inc(pe_filled, 1)
            pe.wait_ge(ranked, k)
            ps = begin(J.at[f"tokens{L}"])
            for q in range(KT):
                last = nc.tensor.matmul(ps[:, 0:2 * ETC], OHR[:, q, :], TV[:, q, :, :].rearrange("p a b -> p (a b)"),
                                        start=(q == 0), stop=(q == KT - 1))
            last.then_inc(pe_filled, 1)
            pe.wait_ge(gates_ready, k)
            for q in range(3):
                ps = begin(J.at[f"gatesT{L}"] + q)
                for t in range(4 * q, min(4 * q + 4, NT)):
                    last = nc.tensor.transpose(ps[0:NE, (t % 4) * T:(t % 4 + 1) * T], GA[:, t, :], ident[0:T, 0:T])
                last.then_inc(pe_filled, 1)
            pe.wait_ge(act_emptied, J.emptied("act", J.at[f"gatesT{L}"] + 2))
            for t in range(NT):
                for b in range(2):
                    ps = begin(J.at[f"ebias{L}"] + 2 * t + b)
                    nc.tensor.matmul(ps[0:T, 0:HC], WT[:, t * T:(t + 1) * T], EB[:, b * HC:(b + 1) * HC],
                                     start=True, stop=True).then_inc(pe_filled, 1)
            m = J.at[f"ebias{L}"] + 19
            pe.wait_ge(act_emptied, J.emptied("act", m))
            pe.wait_ge(dve_emptied, J.emptied("dve", m))

        def turn(L, n, a, wait_in):
            pe.wait_ge(xg_in[L][a], wait_in)
            if L == 1:
                if not isinstance(n, int):
                    pe.wait_ge(xgt_ready[L], n)
                b0 = 2 * a
            else:
                if not isinstance(n, int) or n > 0:
                    pe.wait_ge(xgt_ready[L], n + 1)
                b0 = 0
            for k in range(KC):
                last = nc.tensor.transpose(PS[:, b0 + k // 3, (k % 3) * P:(k % 3 + 1) * P], XG[:, a, k * P:(k + 1) * P], ident)
            last.then_inc(turned_n[L], 1)

        def weights_of(L, n, u0):
            e = nc.tensor.value_load(TAB[0:1, 0, bass.ds(n, 1)], min_val=0, max_val=NE - 1)
            c = copies[u0]
            pe.wait_ge(w_in[0], (e // 2) * (16 * c) + arrived(u0))
            pe.wait_ge(w_in[1], ((e + 1) // 2) * (16 * c) + (arrived(u0 + 1) - 16 * c))
            return e % 2

        transposes(1)
        route(1)
        pe.wait_ge(tab_ready, 1)
        turns1 = nc.tensor.value_load(TAB[0:1, 2, 0:1], min_val=1, max_val=ET_MAX // 2)

        def expert0(n, a):
            slot = weights_of(1, n, U_EW)
            pe.wait_ge(xgt_ready[1], n + 2)
            pe.wait_ge(y_free[1], n + 1)
            for b in range(2):
                for k in range(KC):
                    last = nc.tensor.matmul(PS[:, 4 + 2 * a + b, 0:HC], XGT[:, a, k, :],
                                            WS[:, bass.ds(slot, 1), k * C + b * HC:k * C + (b + 1) * HC].rearrange("p a b -> p (a b)"),
                                            start=(k == 0), stop=(k == KC - 1))
            last.then_inc(y_filled[1], 1)

        pe.drain().then_inc(turned_n[1], 1)
        pe.drain().then_inc(y_filled[1], 1)
        turn(1, 0, 0, 16)
        with nc.tensor.Fori(0, turns1) as i:
            turn(1, i * 2 + 1, 1, i * 16 + 16)
            expert0(i * 2, 0)
            turn(1, i * 2 + 2, 0, i * 16 + 32)
            expert0(i * 2 + 1, 1)
        if STOP <= 3:
            return

        transposes(2)
        xt_ready(2)
        for n, name in enumerate(("q1", "k1", "v1")):
            columns(J.at[name], weights(U_MIX1 + n), XT)
        w = weights(U_MIX1 + 3)
        pe.wait_ge(dve_emptied, J.emptied("dve", J.at["proj1"] - 1))
        for t in range(NT):
            rows(J.at["proj1"] + 2 * t, QK, w, t)

        pe.wait_ge(loops, 1)
        for c, (o, n) in enumerate(CH):
            ps = begin(J.at["deg"] + c)
            for s in range(NT):
                last = nc.tensor.matmul(ps[:, 0:n], onesr[0:T, :], AT[:, s, o:o + n], start=(s == 0), stop=(s == NT - 1))
            last.then_inc(pe_filled, 1)
        pe.wait_ge(deg_root, 2)
        for q in range(3):
            ps = begin(J.at["dinv"] + q)
            for t in range(4 * q, min(4 * q + 4, NT)):
                last = nc.tensor.transpose(ps[0:T, (t % 4) * P:(t % 4 + 1) * P], DB[:, t * T:(t + 1) * T], ident)
            last.then_inc(pe_filled, 1)
        w = weights(U_GCN)
        for t in range(NT):
            rows(J.at["conv1"] + 2 * t, XT, w, t)
        pe.wait_ge(hf_hi, 20)
        pe.wait_ge(hf_used, 20)
        for q in range(KC):
            for c, (o, n) in enumerate(CH):
                ps = begin(J.at["agg1"] + 3 * q + c)
                for s in range(NT):
                    for v in range(2):
                        last = nc.tensor.matmul(ps[:, 0:n], HH[:, v, s, q * P:(q + 1) * P], AT[:, s, o:o + n],
                                                start=(s + v == 0), stop=(s == NT - 1 and v == 1))
                last.then_inc(pe_filled, 1)
        w = weights(U_GCN + 1)
        pe.wait_ge(h1_ready, 18)
        for t in range(NT):
            rows(J.at["conv2"] + 2 * t, XT, w, t)
        pe.wait_ge(hf_used, 40)
        for t in range(NT):
            for b in range(2):
                ps = begin(J.at["agg2"] + 2 * t + b)
                for s in range(NT):
                    for v in range(2):
                        last = nc.tensor.matmul(ps[0:T, 0:HC], AT[:, s, t * T:(t + 1) * T],
                                                HH[:, v, s, b * HC:(b + 1) * HC],
                                                start=(s + v == 0), stop=(s == NT - 1 and v == 1))
                last.then_inc(pe_filled, 1)
        if STOP <= 4:
            return

        transposes(3)
        route(3)
        pe.wait_ge(tab_ready, 2)
        turns3 = nc.tensor.value_load(TAB[0:1, 2, 0:1], min_val=1, max_val=ET_MAX // 2)
        FC = FH // P

        def hidden(n, a):
            slot = weights_of(3, n, U_FF)
            pe.wait_ge(xgt_ready[3], n + 2)
            if not isinstance(n, int):
                pe.wait_ge(hid_summed[3], n)
            for k in range(KC):
                last = nc.tensor.matmul(PS[:, 2 + a, 0:FH], XGT[:, a, k, :],
                                        WS[:, bass.ds(slot, 1), k * FH:(k + 1) * FH].rearrange("p a b -> p (a b)"),
                                        start=(k == 0), stop=(k == KC - 1))
            last.then_inc(hid_filled[3], 1)

        def turn_hidden(n, a):
            pe.wait_ge(hid_ready[3], n + 1)
            pe.wait_ge(ht_ready[3], n + 1)
            for k in range(FC):
                last = nc.tensor.transpose(PS[:, 4, k * P:(k + 1) * P], HR[:, a, k * P:(k + 1) * P], ident)
            last.then_inc(ht_filled[3], 1)

        def expert1(n, a):
            e = nc.tensor.value_load(TAB[0:1, 0, bass.ds(n, 1)], min_val=0, max_val=NE - 1)
            slot = e % 2
            pe.wait_ge(ht_ready[3], n + 2)
            pe.wait_ge(y_free[3], n + 1)
            for b in range(2):
                for k in range(FC):
                    o = KC * FH + k * C + b * HC
                    last = nc.tensor.matmul(PS[:, 5 + b, 0:HC], HT[:, k, :],
                                            WS[:, bass.ds(slot, 1), o:o + HC].rearrange("p a b -> p (a b)"),
                                            start=(k == 0), stop=(k == FC - 1))
            last.then_inc(y_filled[3], 1)

        for progress in (turned_n, y_filled, ht_filled, hid_filled):
            pe.drain().then_inc(progress[3], 1)
        turn(3, 0, 0, 16)
        turn(3, 1, 1, 16)
        hidden(0, 0)
        with nc.tensor.Fori(0, turns3) as i:
            for a in range(2):
                n = i * 2 + a
                turn_hidden(n, a)
                turn(3, n + 2, a, i * 16 + 32)
                hidden(n + 1, 1 - a)
                expert1(n, a)

    @block.scalar
    def _(act):
        def full(m):
            act.wait_ge(pe_filled, J.filled(m))
            return bank(m)

        def transposed(L):
            act.wait_ge(ln_var, L + 1)
            nc.scalar.activation(std, std, ACT.Sqrt).then_inc(ln_std, 1)
            for t in range(NT):
                if L in (1, 3):
                    act.wait_ge(xn_ready, L * NT + t + 1)
                    act.dma_start(xn_d[t * T:(t + 1) * T, :], XN[:, t % XNB, :]).then_inc(xn_out[t % XNB], 16)
                for b in range(2):
                    ps = full(J.at[f"lnt{L}"] + 2 * t + b)
                    nc.scalar.activation(XT[:, 3 * b:3 * b + 3, t * T:(t + 1) * T],
                                         ps[:, 0:3 * T].rearrange("p (k n) -> p k n", k=3), ACT.Copy).then_inc(act_emptied, 1)

        transposed(0)
        def lower_exp(tmp, ps, m_sem):
            nc.scalar.activation(tmp, ps, ACT.Relu, scale=-1.0)
            nc.scalar.drain()
            nc.scalar.activation(tmp, tmp, ACT.Exp, scale=-1.0).then_inc(m_sem, 1)

        for t in range(NT):
            for b in range(2):
                n = 2 * t + b
                ps = full(J.at["kv"] + 4 * t + b)
                if n >= 2:
                    act.wait_ge(dve_emptied, J.emptied("dve", J.at["kv"] + 4 * (t - 1) + b))
                lower_exp(TK[:, n % 2, :], ps[0:T, 0:HC], kexp)
            for b in range(2):
                ps = full(J.at["kv"] + 4 * t + 2 + b)
                nc.scalar.activation(VR[:, t, 3 * b:3 * b + 3, 0:P], ps[0:T, 0:HC].rearrange("p (k n) -> p k n", k=3),
                                     ACT.Copy).then_inc(act_emptied, 1)
        for r in range(18):
            n = CH[r % 3][1]
            ps = full(J.at["q0"] + r)
            if r >= 4:
                act.wait_ge(dve_emptied, J.emptied("dve", J.at["q0"] + r - 4))
            else:
                act.wait_ge(pe_filled, J.filled(J.at["kvsum"] + 5))
            lower_exp(TQ[:, r % 4 // 2, r % 2, 0:n], ps[:, 0:n], qexp)
        act.wait_ge(z_ready, 1)
        for f in range(4):
            nc.scalar.activation(EX[:, f], ZZ[:, f], ACT.Exp).then_inc(e_ready, 1)

        def turned(g):
            for q in range(3):
                r = 3 * g + q
                w = min(4 * q + 4, NT) - 4 * q
                act.wait_ge(tr_filled, 2 + r + 1)
                nc.scalar.activation(AT[:, 4 * q:4 * q + w, g * T:(g + 1) * T],
                                     PS[0:T, 6 + r % 2, 0:w * T].rearrange("p (s n) -> p s n", s=w),
                                     ACT.Copy).then_inc(tr_emptied, 1)

        for g in range(NT):
            act.wait_ge(acc_done, g + 1)
            if g >= 2:
                act.wait_ge(tr_filled, 2 + 3 * (g - 1))
            for c, (o, n) in enumerate(CH):
                nc.scalar.activation(AROW[:, g % 2, o:o + n], PS[0:T, 3 * (g % 2) + c, 0:n], ACT.Copy).then_inc(arow_ready, 1)
            if g >= 1:
                turned(g - 1)
        turned(NT - 1)
        if STOP <= 0:
            return

        def pair(i):
            first = isinstance(i, int)
            if not first:
                act.wait_ge(a2_filled, i * 6)
            nc.scalar.activation(XPS, XT[:, bass.ds(i, 1), :].rearrange("p a n -> p (a n)"), ACT.Copy).then_inc(xp_staged, 1)
            if not first:
                act.wait_ge(f_ready, i * 2)
            for r in range(5):
                act.wait_ge(g56_filled, i * 15 + r + 1)
                if r == 0 and not first:
                    act.wait_ge(num_used, i * 4 - 4)
                ps = PS[0:T, 5 + r % 2, :].rearrange("p (t c) -> p t c", t=2)
                for j in range(2):
                    nc.scalar.activation(FT[:, 2 * r:2 * r + 2, j, 0:D], ps[:, :, j * D:(j + 1) * D], ACT.Copy)
                nc.scalar.activation(RES[:, bass.ds(i % 2, 1), 2 * r:2 * r + 2, :].rearrange("p a t c -> p (a t) c"),
                                     ps[:, :, P:], ACT.Copy)
                nc.scalar.drain().then_inc(g56_emptied, 1)
            for j in range(2):
                if not first:
                    act.wait_ge(b1_ready, i * 40)
                for c, (o, n) in enumerate(CH):
                    act.wait_ge(a2_filled, i * 6 + 3 * j + c + 1)
                    nc.scalar.activation(A2B[:, j, o:o + n], PS[0:T, 7, 0:n], ACT.Copy).then_inc(a2_emptied, 1)
            for j in range(2):
                act.wait_ge(f_ready, i * 2 + j + 1)
                if not first:
                    act.wait_ge(accb_filled, i * 20)
                nc.scalar.activation(PF[:, j, :, 0, :], F, ACT.Copy).then_inc(pf_hi, 1)
            for r in range(NT):
                act.wait_ge(g56_filled, i * 15 + 5 + r + 1)
                if not first:
                    act.wait_ge(num_ready, i * 4)
                nc.scalar.activation(YA[:, r].rearrange("p a b c -> p (a b c)"), PS[0:T, 5 + (r + 1) % 2, 0:4 * DW],
                                     ACT.Copy).then_inc(g56_emptied, 1)
            for g in range(4):
                for b in range(5):
                    act.wait_ge(accb_filled, i * 20 + 5 * g + b + 1)
                    if b == 0 and (g >= 2 or not first):
                        act.wait_ge(y_used, i * 4 + g - 1)
                    nc.scalar.activation(Y1[:, g % 2, b, :], PS[0:T, b, 0:4 * DW], ACT.Copy).then_inc(y_emptied, 1)

        act.wait_ge(wbd_ready, 64)
        pair(0)
        with nc.scalar.Fori(1, NP) as i:
            pair(i)
        if STOP <= 1:
            return

        def route(L, k):
            act.wait_ge(gexp_in, k)
            nc.scalar.activation(RS[:, 1], RS[:, 0], ACT.Exp).then_inc(gexp_out, 1)
            for q in range(3):
                ps = full(J.at[f"gatesT{L}"] + q)
                w = (min(4 * q + 4, NT) - 4 * q) * T
                nc.scalar.activation(WT[:, 4 * q * T:4 * q * T + w], ps[0:NE, 0:w], ACT.Copy).then_inc(act_emptied, 1)

        def columns_of(L, n, a):
            act.wait_ge(turned_n[L], n + 2)
            b0 = 2 * a if L == 1 else 0
            if not isinstance(n, int):
                act.wait_ge(y_filled[L] if L == 1 else hid_filled[L], n)
            for b in range(2):
                nc.scalar.activation(XGT[:, a, 3 * b:3 * b + 3, :], PS[:, b0 + b, 0:3 * P].rearrange("p (k n) -> p k n", k=3),
                                     ACT.Copy)
            nc.scalar.drain().then_inc(xgt_ready[L], 1)

        def store(L, n, a, i):
            act.wait_ge(y_filled[L], n + 2)
            act.wait_ge(ys_out[L][a], i * 16 + 16)
            b0 = 4 + 2 * a if L == 1 else 5
            for b in range(2):
                nc.scalar.activation(YS[:, a, b * HC:(b + 1) * HC], PS[:, b0 + b, 0:HC], ACT.Copy)
            nc.scalar.drain().then_inc(y_free[L], 1)
            act.wait_ge(y_free[L], n + (3 if L == 1 else 2))
            act.dma_start(y_d[bass.ds(n * P, P), :], YS[:, a, :]).then_inc(ys_out[L][a], 16)

        transposed(1)
        route(1, 1)
        act.wait_ge(tab_ready, 1)
        turns1 = nc.scalar.value_load(TAB[0:1, 2, 0:1], min_val=1, max_val=ET_MAX // 2)
        act.wait_ge(y_cleared, 16)
        nc.scalar.drain().then_inc(y_free[1], 2)
        nc.scalar.drain().then_inc(xgt_ready[1], 1)
        for b in range(2):
            nc.scalar.drain().then_inc(ys_out[1][b], 16)
        columns_of(1, 0, 0)
        with nc.scalar.Fori(0, turns1) as i:
            columns_of(1, i * 2 + 1, 1)
            store(1, i * 2, 0, i)
            columns_of(1, i * 2 + 2, 0)
            store(1, i * 2 + 1, 1, i)
        if STOP <= 3:
            return

        transposed(2)
        for r in range(18):
            q, c = r // 3, r % 3
            o, n = CH[c]
            ps = full(J.at["q1"] + r)
            nc.scalar.activation(QK[:, q, o:o + n], ps[:, 0:n], ACT.Copy, accum_out=SQ[:, 0, q, c:c + 1])
            nc.scalar.activation(JK[:, r % 2, 0:n], ps[:, 0:n], ACT.Square, accum_out=SQ[:, 2, q, c:c + 1])
            nc.scalar.drain().then_inc(act_emptied, 1)
        for r in range(18):
            q, c = r // 3, r % 3
            o, n = CH[c]
            ps = full(J.at["k1"] + r)
            if r >= 2:
                act.wait_ge(k2_used, r - 1)
            nc.scalar.activation(K2[:, r % 2, 0:n], ps[:, 0:n], ACT.Square, accum_out=SQ[:, 3, q, c:c + 1])
            nc.scalar.activation(JK[:, r % 2, 0:n], ps[:, 0:n], ACT.Copy, accum_out=SQ[:, 1, q, c:c + 1])
            nc.scalar.drain().then_inc(act_emptied, 1)
        act.wait_ge(norm_in, 1)
        nc.scalar.activation(SC[:, 0:2], S4[:, 2:4], ACT.Sqrt).then_inc(norm_out, 1)
        act.wait_ge(deg_sum, 1)
        nc.scalar.activation(DB, DB, ACT.Sqrt).then_inc(deg_root, 1)

        def scaled_rows(name, k):
            for r in range(20):
                t, b = r // 2, r % 2
                ps = full(J.at[name] + r)
                if 20 * k + r >= 2:
                    act.wait_ge(hf_used, 20 * k + r - 1)
                nc.scalar.activation(HF[:, b, :], ps[0:T, 0:HC], ACT.Copy, scale=DT[:, t:t + 1]).then_inc(act_emptied, 1)
                nc.scalar.drain()
                nc.scalar.activation(HH[:, 0, t, b * HC:(b + 1) * HC], HF[:, b, :], ACT.Copy).then_inc(hf_hi, 1)

        act.wait_ge(dve_emptied, J.emptied("dve", J.at["dinv"] + 2))
        scaled_rows("conv1", 0)
        act.wait_ge(misc_in, 16)
        for r in range(18):
            q, c = r // 3, r % 3
            o, n = CH[c]
            act.wait_ge(dve_emptied, J.emptied("dve", J.at["agg1"] + r))
            nc.scalar.activation(XT[:, q, o:o + n], TA[:, r % 2, 0:n], ACT.Relu, bias=B1C[:, q:q + 1]).then_inc(h1_ready, 1)
        scaled_rows("conv2", 1)
        if STOP <= 4:
            return

        transposed(3)
        route(3, 2)
        act.wait_ge(tab_ready, 2)
        turns3 = nc.scalar.value_load(TAB[0:1, 2, 0:1], min_val=1, max_val=ET_MAX // 2)
        nc.scalar.drain().then_inc(y_free[3], 1)
        nc.scalar.drain().then_inc(xgt_ready[3], 1)
        nc.scalar.drain().then_inc(ht_ready[3], 1)
        for b in range(2):
            nc.scalar.drain().then_inc(ys_out[3][b], 16)

        def gelu(n, a):
            act.wait_ge(hid_summed[3], n + 2)
            nc.scalar.activation(HR[:, a, :], HR[:, a, :], ACT.Gelu).then_inc(hid_ready[3], 1)

        def hidden_columns(n):
            act.wait_ge(ht_filled[3], n + 2)
            act.wait_ge(y_filled[3], n + 1)
            nc.scalar.activation(HT, PS[:, 4, 0:FH].rearrange("p (k n) -> p k n", k=FH // P), ACT.Copy).then_inc(ht_ready[3], 1)

        columns_of(3, 0, 0)
        columns_of(3, 1, 1)
        gelu(0, 0)
        with nc.scalar.Fori(0, turns3) as i:
            for a in range(2):
                n = i * 2 + a
                hidden_columns(n)
                columns_of(3, n + 2, a)
                gelu(n + 1, 1 - a)
                store(3, n, a, i)

    @block.vector
    def _(dve):
        def full(m):
            dve.wait_ge(pe_filled, J.filled(m))
            return bank(m)

        V = nc.vector

        def layer_norm(L):
            for t in range(NT):
                for b in range(2):
                    V.bn_stats(stats[:, t, 6 * b:6 * b + 6], X[:, t, b * HC:(b + 1) * HC])
            V.drain()
            for t in range(NT):
                V.bn_aggr(mv[:, t, :], stats[:, t, :])
            V.drain()
            V.tensor_scalar(std, mv[:, :, 1], LN_EPS, None, ALU.add).then_inc(ln_var, 1)
            dve.wait_ge(ln_std, L + 1)
            V.reciprocal(rstd, std)
            V.drain()
            for t in range(NT):
                if t >= XNB:
                    dve.wait_ge(pe_filled, J.filled(J.at[f"lnt{L}"] + 2 * (t - XNB) + 1))
                    if L in (1, 3):
                        dve.wait_ge(xn_out[t % XNB], xn_stores(L, t % XNB) - xn_stores(1, t % XNB) + 16 * (t // XNB))
                V.tensor_scalar(XN[:, t % XNB, :], X[:, t, :], mv[:, t, 0:1], rstd[:, t:t + 1], ALU.subtract,
                                ALU.mult).then_inc(xn_ready, 1)

        V.memset(ones, 1.0)
        dve.wait_ge(consts, 6)
        V.tensor_copy(pref, pref_i)
        V.tensor_copy(pcol, pcol_i)
        V.tensor_copy(k128, k128_i)
        V.tensor_copy(tq, tq_i)
        V.tensor_copy(io128, io128_i)
        V.drain()
        V.tensor_scalar(before, io128[:, 0:T], pcol[0:T, :], None, ALU.is_gt)
        V.tensor_copy(onesr, ones)
        dve.wait_ge(e_in, 32)
        V.tensor_copy(EF, EI).then_inc(edge_f, 1)
        ps = full(0)
        V.tensor_copy(ES.rearrange("p a b -> p (a b)"), ps[0:T, 0:320]).then_inc(dve_emptied, 1)
        dve.wait_ge(x_in, 16)
        layer_norm(0)
        V.memset(VR[:, :, :, P:], 1.0)
        V.memset(KVB, 0.0)
        for t in range(NT):
            for b in range(2):
                n = 2 * t + b
                ps = full(J.at["kv"] + 4 * t + b)
                dve.wait_ge(kexp, n + 1)
                V.scalar_tensor_tensor(out=KR[:, t, b * HC:(b + 1) * HC], in0=ps[0:T, 0:HC], scalar=0.0,
                                       in1=TK[:, n % 2, :], op0=ALU.max, op1=ALU.add).then_inc(dve_emptied, 1)
        for p in range(NP):
            ps = full(J.at["kvsum"] + p)
            for r in range(2):
                rr = slice(r * D, (r + 1) * D)
                V.tensor_copy(KVB[rr, p, r * D:(r + 1) * D], ps[rr, r * D:(r + 1) * D])
                V.tensor_scalar(KSB[rr, p, :], ones[rr, :], ps[rr, P:P + 1], None, ALU.mult)
            V.drain()
            V.memset(KSB[0:D, p, D:], 0.0)
            V.memset(KSB[D:P, p, 0:D], 0.0)
            V.drain().then_inc(dve_emptied, 1)
        for r in range(18):
            o, n = CH[r % 3]
            ps = full(J.at["q0"] + r)
            dve.wait_ge(qexp, r + 1)
            V.scalar_tensor_tensor(out=QT[:, r // 3, o:o + n], in0=ps[:, 0:n], scalar=0.0, in1=TQ[:, r % 4 // 2, r % 2, 0:n],
                                   op0=ALU.max, op1=ALU.add).then_inc(dve_emptied, 1)
        V.drain()
        for r in range(18):
            p, c = r // 3, r % 3
            o, n = CH[c]
            m = J.at["lin"] + 2 * r
            ps = full(m)
            V.reciprocal(TQ[:, 0, r % 2, 0:n], ps[:, 0:n]).then_inc(dve_emptied, 1)
            ps = full(m + 1)
            V.drain()
            V.tensor_tensor(QT[:, p, o:o + n], ps[:, 0:n], TQ[:, 0, r % 2, 0:n], ALU.mult).then_inc(dve_emptied, 1)

        def add_rows(name, n=20):
            for r in range(n):
                t, b = r // 2, r % 2
                ps = full(J.at[name] + r)
                xs = X[:, t, b * HC:(b + 1) * HC]
                V.tensor_tensor(xs, ps[0:T, 0:HC], xs, ALU.add).then_inc(dve_emptied, 1)

        V.drain()
        add_rows("proj0")
        dve.wait_ge(mix_bias, 16)
        V.drain()
        V.tensor_tensor(X, X, BB.unsqueeze(1).to_broadcast([T, NT, C]), ALU.add)
        V.drain()
        V.memset(vz, 0.0)
        ps = full(J.at["attn_vec"])
        V.tensor_copy(vv, ps[:, 0:2 * H]).then_inc(dve_emptied, 1)
        V.drain()
        V.tensor_scalar(vvn, vv, -1.0, None, ALU.mult)
        vzf = vz.rearrange("p a b -> p (a b)")
        step = 2 * H + 2
        for side in range(2):
            for r in range(2):
                o = side * H + r
                V.tensor_copy(vzf[r * D:(r + 1) * D, o:o + 5 * step + 1:step], vv[r * D:(r + 1) * D, o:o + H - 1:2])
        V.drain().then_inc(vz_ready, 1)
        ps = full(J.at["node_att"])
        V.tensor_copy(GT.rearrange("p a b -> p (a b)"), ps[0:T, 0:NT * 2 * H]).then_inc(dve_emptied, 1)
        for c, (o, n) in enumerate(CH):
            ps = full(J.at["att_rows"] + c)
            V.tensor_reduce(gmax[:, c:c + 1], ps[0:H, 0:n], AX.X, ALU.max).then_inc(dve_emptied, 1)
        V.drain()
        V.tensor_reduce(gmax[:, 3:4], gmax[:, 0:3], AX.X, ALU.max)
        V.drain()
        V.tensor_scalar(gdiag, ident[0:H, 0:H], gmax[:, 3:4], None, ALU.mult).then_inc(gdiag_ready, 1)
        ps = full(J.at["att_max"])
        V.tensor_copy(GB, ps[0:T, 0:H]).then_inc(dve_emptied, 1)
        V.drain()
        gb = GB.unsqueeze(1).to_broadcast([T, NT, H])
        V.tensor_tensor(ZZ[:, 0], GT[:, :, 0:H], gb, ALU.subtract)
        V.tensor_tensor(ZZ[:, 2], GT[:, :, H:], gb, ALU.add)
        V.drain()
        V.tensor_scalar(ZZ[:, 1], ZZ[:, 0], SLOPE, None, ALU.mult)
        V.tensor_scalar(ZZ[:, 3], ZZ[:, 2], SLOPE - 1.0, 0.0, ALU.mult, ALU.min)
        V.drain()
        V.tensor_scalar(ZZ[:, 2], ZZ[:, 2], 1.0 - SLOPE, 0.0, ALU.mult, ALU.min)
        V.drain().then_inc(z_ready, 1)

        dve.wait_ge(consts, 9)
        V.memset(zeros, 0.0)
        V.tensor_copy(iota, iota_i)
        V.tensor_copy(gidx, gidx_i)
        V.tensor_copy(tidx, tidx_i)
        for a in range(2):
            V.tensor_reduce(mnx[:, 0, a:a + 1], EF[:, 2 + a, :], AX.X, ALU.min)
            V.tensor_reduce(mnx[:, 1, a:a + 1], EF[:, 2 + a, :], AX.X, ALU.max)
        V.drain()
        for a in range(2):
            V.tensor_scalar(hit[:, a, 0, :], gidx[:, 0, :], mnx[:, 1, a:a + 1], None, ALU.is_le)
        V.drain()
        for a in range(2):
            V.scalar_tensor_tensor(out=hit[:, a, 1, :], in0=gidx[:, 1, :], scalar=mnx[:, 0, a:a + 1],
                                   in1=hit[:, a, 0, :], op0=ALU.is_gt, op1=ALU.mult)
        V.drain()
        V.tensor_scalar(mnx[:, 0, :], tidx, -1.0, float(ET), ALU.mult, ALU.add)
        V.tensor_scalar(mnx[:, 1, :], tidx, 1.0, None, ALU.add)
        V.drain()
        for a in range(2):
            V.tensor_scalar(hit[:, a, 0, :], hit[:, a, 1, :], mnx[:, 0, a:a + 1], None, ALU.mult)
        V.drain()
        for a in range(2):
            V.tensor_scalar(hit[:, a, 1, :], hit[:, a, 1, :], mnx[:, 1, a:a + 1], None, ALU.mult)
        V.drain().then_inc(ranged, 1)
        dve.wait_ge(tr_filled, 1)
        V.tensor_reduce(rng, PS[0:2 * NT, 7, 0:160], AX.X, ALU.max).then_inc(ranged, 1)
        dve.wait_ge(tr_filled, 2)
        V.tensor_copy(span[:, 0:2, :].rearrange("p a b -> p (a b)"), PS[0:1, 7, 256:256 + 2 * NT])
        V.drain()
        V.tensor_tensor(span[:, 3, :], span[:, 0, :], span[:, 1, :], ALU.add)
        V.tensor_scalar(span[:, 2, :], span[:, 0, :], -1.0, float(ET), ALU.mult, ALU.add)
        V.drain()
        V.tensor_scalar(span[:, 3, :], span[:, 3, :], float(-ET), 1.0, ALU.add, ALU.max)
        V.drain()
        V.tensor_tensor(turns, span[:, 3, :].unsqueeze(2).to_broadcast([1, NT, ET // SLOTS]),
                        iota[0:1, 0:ET:SLOTS].unsqueeze(1).to_broadcast([1, NT, ET // SLOTS]), ALU.is_gt)
        V.drain()
        V.tensor_reduce(span[:, 3, :], turns, AX.X, ALU.add)
        V.drain()
        V.tensor_scalar(span[:, 6, :], span[:, 3, :], float(-SLOTS), float(ET), ALU.mult, ALU.add)
        V.memset(span[:, 5, :], 0.0)
        V.drain()
        V.tensor_tensor(span[:, 2, :], span[:, 2, :], span[:, 6, :], ALU.min)
        V.tensor_tensor_scan(out=span[:, 4, :], data0=span[:, 3, :], data1=span[:, 5, :], initial=0.0, op0=ALU.add, op1=ALU.add)
        V.drain()
        V.tensor_tensor(span[:, 4, :], span[:, 4, :], span[:, 3, :], ALU.subtract)
        V.drain()
        V.tensor_copy(table, span[:, 2:5, :])
        V.drain().then_inc(table_ready, 1)
        for g in range(NT):
            t0 = nc.vector.value_load(table[0:1, 0, g:g + 1], min_val=0, max_val=ET - SLOTS)
            n = nc.vector.value_load(table[0:1, 1, g:g + 1], min_val=1, max_val=ET // SLOTS)
            done_before = nc.vector.value_load(table[0:1, 2, g:g + 1], min_val=0, max_val=ET * NT // SLOTS)
            if g == 0:
                nc.vector.engine_nop().then_inc(oh_free, SLOTS)
            with nc.vector.Fori(0, n) as j:
                u = done_before + j
                tile = nc.s_assert_within(t0 + j * SLOTS, 0, ET - SLOTS, skip_runtime_bounds_check_because=
                                          "a span's first tile is at most ET less the tiles of its turns")
                for k in range(SLOTS):
                    dve.wait_ge(oh_free, u * SLOTS + k + 1)
                    V.tensor_scalar(OHD[:, k, :], iota[0:T, g * T:(g + 1) * T], ES[:, 1, bass.ds(tile + k, 1)],
                                    None, ALU.is_equal).then_inc(oh_ready, 1)
                    V.tensor_scalar(OHS[:, k, :], iota[0:T, :], ES[:, 0, bass.ds(tile + k, 1)],
                                    None, ALU.is_equal).then_inc(oh_ready, 1)

        dve.wait_ge(tr_filled, 2 + 3 * NT)
        V.memset(WBD, 0.0).then_inc(wbd_zero, 1)
        V.memset(VRS, 0.0)
        V.memset(FT[:, :, :, D:D + 1], 1.0)
        V.memset(FT[:, :, :, D + 1:], 0.0)
        V.drain()
        dve.wait_ge(e_ready, 4)
        dve.wait_ge(tr_emptied, 3 * NT)

        def final(i, g):
            j, half = g // 2, g % 2
            h = i * 2 + j
            t0 = 5 * half
            y = NUM[:, g % 2]
            dve.wait_ge(num_ready, i * 4 + g + 1)
            V.tensor_scalar(RD, y[:, :, D:D + 1], TINY, None, ALU.max)
            V.drain()
            V.reciprocal(RD, RD)
            V.drain()
            V.tensor_tensor(y[:, :, 0:D], y[:, :, 0:D], RD.to_broadcast([T, 5, D]), ALU.mult)
            V.drain()
            V.tensor_tensor(y[:, :, 0:D], y[:, :, 0:D],
                            RES[:, bass.ds(i % 2, 1), t0:t0 + 5, j * D:(j + 1) * D].rearrange("p a t c -> p (a t) c"), ALU.add)
            V.drain()
            xs = X[:, t0:t0 + 5, bass.ds(h * D, D)]
            V.scalar_tensor_tensor(out=xs, in0=y[:, :, 0:D], scalar=0.0, in1=xs, op0=ALU.max, op1=ALU.add).then_inc(num_used, 1)

        def pair(i):
            first = isinstance(i, int)
            if not first:
                dve.wait_ge(a2_filled, i * 6)
            for j in range(2):
                V.tensor_scalar(VRS[j * D:(j + 1) * D, j, :], ones[j * D:(j + 1) * D, 0:T],
                                vvn[j * D:(j + 1) * D, bass.ds(i * 2 + j + H, 1)], None, ALU.mult).then_inc(vrs_ready, 1)
            dve.wait_ge(g56_emptied, i * 15 + 5)
            for j in range(2):
                h = i * 2 + j
                for f in range(2):
                    V.tensor_tensor(F[:, :, f * DW:(f + 1) * DW], FT[:, :, j, :],
                                    EX[:, f, :, bass.ds(h, 1)].to_broadcast([T, NT, DW]), ALU.mult)
                V.drain().then_inc(f_ready, 1)
                dve.wait_ge(pf_hi, i * 2 + j + 1)
                V.tensor_tensor(PF[:, j, :, 1, :], F, PF[:, j, :, 0, :].bitcast(F32), ALU.subtract)
                V.drain().then_inc(pf_ready, 1)
            for g in range(4):
                j, half = g // 2, g % 2
                h = i * 2 + j
                dve.wait_ge(a2_emptied, i * 6 + 3 * j + 3)
                for s in range(NT):
                    n = g * 10 + s - BSLOTS
                    gg, ss = n // 10, n % 10
                    if not first or n >= 0:
                        if ss == 9:
                            dve.wait_ge(accb_filled, i * 20 + 5 * (gg + 1))
                        else:
                            dve.wait_ge(b1_used, i * 36 + 9 * gg + ss + 1)
                    V.scalar_tensor_tensor(out=B1[:, (g * 10 + s) % BSLOTS, :], in0=A2B[:, j, half * RH:(half + 1) * RH],
                                           scalar=GT[:, s, bass.ds(h, 1)], in1=AT[:, s, half * RH:(half + 1) * RH].bitcast(F32),
                                           op0=ALU.is_le, op1=ALU.mult).then_inc(b1_ready, 1)
                if g:
                    final(i, g - 1)
                elif not first:
                    final(i - 1, 3)

        pair(0)
        with nc.vector.Fori(1, NP) as i:
            pair(i)
        final(NP - 1, 3)
        V.drain().then_inc(stage_done, 1)
        if STOP <= 1:
            V.drain().then_inc(done, 1)
            return

        def route(L, k, normalised):
            ps = full(J.at[f"route{L}"])
            g = lambda n: RS[:, n]
            r = lambda n: R1[:, n, :]
            spread = lambda n: R1[:, n, :].unsqueeze(2).to_broadcast([T, NT, NE])
            prefb = pref.unsqueeze(1).to_broadcast([T, NT, NE])

            def step(ins):
                V.drain()

            step(V.tensor_tensor(g(0), ps[0:T, 0:NT * NE].rearrange("p (t e) -> p t e", e=NE),
                                 RB.unsqueeze(1).to_broadcast([T, NT, NE]), ALU.add).then_inc(dve_emptied, 1))
            step(V.tensor_reduce(r(0), g(0), AX.X, ALU.max))
            step(V.tensor_tensor(g(0), g(0), spread(0), ALU.subtract))
            V.drain().then_inc(gexp_in, 1)
            dve.wait_ge(gexp_out, k)
            step(V.tensor_reduce(r(1), g(1), AX.X, ALU.add))
            step(V.reciprocal(r(2), r(1)))
            step(V.tensor_tensor(g(2), g(1), spread(2), ALU.mult))
            src_p = 2
            for n in range(2):
                step(V.tensor_reduce(r(3 + n), g(src_p), AX.X, ALU.max))
                step(V.tensor_tensor(g(3), g(src_p), spread(3 + n), ALU.is_equal))
                step(V.tensor_tensor(g(4), g(3), prefb, ALU.mult))
                step(V.tensor_reduce(r(5), g(4), AX.X, ALU.max))
                if n == 1:
                    step(V.tensor_copy(g(9), g(5)))
                step(V.tensor_tensor(g(5), prefb, spread(5), ALU.is_equal))
                if n == 0:
                    step(V.tensor_tensor(g(6), g(5), g(2), ALU.mult))
                    step(V.scalar_tensor_tensor(out=g(7), in0=g(5), scalar=-2.0, in1=g(2), op0=ALU.mult, op1=ALU.add))
                    src_p = 7
                else:
                    step(V.tensor_tensor(g(8), g(5), g(2), ALU.mult))
            step(V.tensor_tensor(GA, g(6), g(8), ALU.add))
            if normalised:
                step(V.tensor_tensor(r(6), r(3), r(4), ALU.add))
                step(V.tensor_scalar(r(6), r(6), 1e-9, None, ALU.add))
                step(V.reciprocal(r(7), r(6)))
                step(V.tensor_tensor(GA, GA, spread(7), ALU.mult))
                for n in (3, 4):
                    step(V.tensor_tensor(r(n), r(n), r(7), ALU.mult))
            V.drain().then_inc(gates_ready, 1)

            step(V.tensor_tensor(SEL, g(9), g(5), ALU.add))
            V.memset(SELB[:, 0, :], 0.0)
            V.drain()
            for t in range(NT):
                step(V.tensor_tensor(SELB[:, t + 1, :], SELB[:, t, :], SEL[:, t, :], ALU.add))
            V.drain().then_inc(sel_ready, 1)
            ps = full(J.at[f"rank{L}"])
            n = NT * NE
            V.tensor_copy(g(0), ps[0:T, 0:n].rearrange("p (t e) -> p t e", e=NE))
            step(V.tensor_copy(CNT, ps[0:T, n:n + NE]).then_inc(dve_emptied, 1))
            step(V.tensor_tensor(CG, CNT.unsqueeze(2).to_broadcast([T, NE, NT]), k128[:, 0:NT].unsqueeze(1).to_broadcast([T, NE, NT]), ALU.is_gt))
            step(V.tensor_reduce(EB4[:, 0, :], CG, AX.X, ALU.add))
            step(V.tensor_scalar(EB4[:, 0, :], EB4[:, 0, :], 1.0, None, ALU.max))
            V.memset(EB4[:, 3, :], 0.0)
            V.drain()
            step(V.tensor_tensor_scan(out=EB4[:, 1, :], data0=EB4[:, 0, :], data1=EB4[:, 3, :], initial=0.0, op0=ALU.add, op1=ALU.add))
            step(V.tensor_tensor(EB4[:, 2, :], EB4[:, 1, :], EB4[:, 0, :], ALU.subtract))
            step(V.tensor_scalar(EB4[:, 3, :], EB4[:, 2, :], float(P), None, ALU.mult))
            step(V.tensor_tensor(g(0), g(0), EB4[:, 3, :].unsqueeze(1).to_broadcast([T, NT, NE]), ALU.add))
            V.tensor_tensor(g(3), g(0), g(9), ALU.mult)
            step(V.tensor_tensor(g(4), g(0), g(5), ALU.mult))
            for n in range(2):
                V.tensor_reduce(POS[:, :, n:n + 1], g(3 + n), AX.X, ALU.add)
            V.drain()
            pos = POS.rearrange("p t k -> p (t k)")
            step(V.tensor_tensor(GE, pos.unsqueeze(2).to_broadcast([T, KT, ETC + 1]),
                                 k128[:, 0:ETC + 1].unsqueeze(1).to_broadcast([T, KT, ETC + 1]), ALU.is_ge))
            step(V.tensor_reduce(TL, GE[:, :, 1:], AX.X, ALU.add))
            V.scalar_tensor_tensor(out=TL, in0=TL, scalar=float(-P), in1=pos, op0=ALU.mult, op1=ALU.add)
            step(V.tensor_tensor(OT, GE[:, :, 0:ETC], GE[:, :, 1:], ALU.subtract))
            for q in range(KT):
                V.tensor_scalar(OHR[:, q, :], io128, TL[:, q:q + 1], None, ALU.is_equal)
            V.tensor_scalar(TV[:, :, 1, :], OT, pcol[0:T, :], None, ALU.mult)
            for n in range(2):
                ot = OT.rearrange("p (t k) e -> p t k e", k=2)[:, :, n, :]
                V.tensor_tensor(TV[:, :, 0, :].rearrange("p (t k) e -> p t k e", k=2)[:, :, n, :], ot,
                                tq.unsqueeze(2).to_broadcast([T, NT, ETC]), ALU.mult)
            V.drain().then_inc(ranked, 1)
            one = lambda n: XT1[:, n, :]
            kk = k128[0:1, :]
            step(V.tensor_tensor(XE, EB4[0:1, 3, :].unsqueeze(1).to_broadcast([1, ETC, NE]),
                                 kk[:, 0:ETC].unsqueeze(2).to_broadcast([1, ETC, NE]), ALU.is_le))
            V.memset(XT1, 0.0)
            V.drain()
            step(V.tensor_reduce(one(0), XE, AX.X, ALU.add))
            V.tensor_copy(one(1)[:, 0:NE], EB4[0:1, 2, :])
            step(V.tensor_scalar(one(0), one(0), -1.0, None, ALU.add))
            step(V.tensor_scalar(one(3)[:, 0:1], EB4[0:1, 1, NE - 1:NE], float(P // 2), None, ALU.mult))
            step(V.tensor_scalar(one(3)[:, 1:1 + ET_MAX // 2], kk[:, 0:ET_MAX // 2], one(3)[:, 0:1], None, ALU.is_lt))
            step(V.tensor_reduce(one(2)[:, 0:1], one(3)[:, 1:1 + ET_MAX // 2], AX.X, ALU.add))
            step(V.tensor_copy(TAB, XT1[:, 0:3, :]))
            ps = full(J.at[f"tokens{L}"])
            step(V.tensor_scalar(TOKF, ps[:, 0:ETC], float(T), None, ALU.mult))
            V.tensor_tensor(TOK, TOKF, ps[:, ETC:2 * ETC], ALU.add).then_inc(dve_emptied, 1)
            V.drain().then_inc(tab_ready, 1)
            add_rows(f"ebias{L}")
            V.drain()

        def gather_sum(L):
            for q in range(KT):
                t, n = q // 2, q % 2
                dve.wait_ge(yg_in[L][n], 16 * (t + 1))
                V.scalar_tensor_tensor(out=X[:, t, :], in0=YG[:, n, :], scalar=R1[:, 3 + n, t:t + 1], in1=X[:, t, :],
                                       op0=ALU.mult, op1=ALU.add).then_inc(yg_used[L], 1)
                dve.wait_ge(yg_used[L], q + 1)

        layer_norm(1)
        dve.wait_ge(small_in, 48)
        route(1, 1, True)
        gather_sum(1)
        V.drain().then_inc(stage_done, 1)
        if STOP <= 3:
            V.drain().then_inc(done, 1)
            return

        layer_norm(2)
        for r in range(18):
            q, c = r // 3, r % 3
            o, n = CH[c]
            dve.wait_ge(act_emptied, J.emptied("act", J.at["k1"] + r))
            V.tensor_tensor(QK[:, q, o:o + n], QK[:, q, o:o + n], K2[:, r % 2, 0:n], ALU.mult).then_inc(k2_used, 1)
        V.tensor_reduce(S4, SQ, AX.X, ALU.add)
        V.drain()
        V.drain().then_inc(norm_in, 1)
        dve.wait_ge(norm_out, 1)
        V.tensor_tensor(SC[:, 2], SC[:, 0], SC[:, 1], ALU.mult)
        V.tensor_tensor(SC[:, 3], S4[:, 0], S4[:, 1], ALU.mult)
        V.drain()
        V.scalar_tensor_tensor(out=SC[:, 4], in0=SC[:, 2], scalar=float(N), in1=SC[:, 3], op0=ALU.mult, op1=ALU.add)
        V.drain()
        V.tensor_tensor(SC[:, 4], SC[:, 4], SC[:, 1], ALU.mult)
        V.drain()
        V.reciprocal(SC[:, 5], SC[:, 4])
        V.drain()
        for r in range(18):
            q, c = r // 3, r % 3
            o, n = CH[c]
            ps = full(J.at["v1"] + r)
            V.scalar_tensor_tensor(out=QK[:, q, o:o + n], in0=ps[:, 0:n], scalar=SC[:, 5, q:q + 1], in1=QK[:, q, o:o + n],
                                   op0=ALU.mult, op1=ALU.mult).then_inc(dve_emptied, 1)

        V.drain()
        dve.wait_ge(mix_bias, 48)
        for b in range(2):
            V.tensor_tensor(X, X, BB1[:, b, :].unsqueeze(1).to_broadcast([T, NT, C]), ALU.add)
            V.drain()
        add_rows("proj1")
        for t in range(NT):
            d = AT[:, t, t * T:(t + 1) * T]
            V.tensor_tensor(d, d.bitcast(F32), ident[0:T, 0:T], ALU.add)
        V.drain().then_inc(loops, 1)
        V.drain().then_inc(stage_done, 1)
        for c, (o, n) in enumerate(CH):
            ps = full(J.at["deg"] + c)
            V.tensor_copy(DB[:, o:o + n], ps[:, 0:n]).then_inc(dve_emptied, 1)
        V.drain().then_inc(deg_sum, 1)
        dve.wait_ge(deg_root, 1)
        V.reciprocal(DB, DB).then_inc(deg_root, 1)
        for q in range(3):
            ps = full(J.at["dinv"] + q)
            w = min(4 * q + 4, NT) - 4 * q
            V.tensor_copy(DT[:, 4 * q:4 * q + w].unsqueeze(2), ps[0:T, 0:w * P].rearrange("p (t n) -> p t n", t=w)[:, :, 0:1]).then_inc(dve_emptied, 1)

        def low_parts(k):
            for r in range(20):
                t, b = r // 2, r % 2
                dve.wait_ge(hf_hi, 20 * k + r + 1)
                V.tensor_tensor(HH[:, 1, t, b * HC:(b + 1) * HC], HF[:, b, :],
                                HH[:, 0, t, b * HC:(b + 1) * HC].bitcast(F32), ALU.subtract).then_inc(hf_used, 1)

        low_parts(0)
        for r in range(18):
            o, n = CH[r % 3]
            ps = full(J.at["agg1"] + r)
            if r >= 2:
                dve.wait_ge(h1_ready, r - 1)
            V.tensor_tensor(TA[:, r % 2, 0:n], ps[:, 0:n], DB[:, o:o + n], ALU.mult).then_inc(dve_emptied, 1)
        low_parts(1)
        for r in range(20):
            t, b = r // 2, r % 2
            ps = full(J.at["agg2"] + r)
            xs = X[:, t, b * HC:(b + 1) * HC]
            V.scalar_tensor_tensor(out=xs, in0=ps[0:T, 0:HC], scalar=DT[:, t:t + 1], in1=xs, op0=ALU.mult,
                                   op1=ALU.add).then_inc(dve_emptied, 1)
        V.drain().then_inc(stage_done, 1)
        if STOP <= 4:
            V.drain().then_inc(done, 1)
            return

        layer_norm(3)
        dve.wait_ge(small_in, 48 + 64)
        route(3, 2, False)
        turns3 = nc.vector.value_load(TAB[0:1, 2, 0:1], min_val=1, max_val=ET_MAX // 2)

        def hidden_bias(n, a):
            dve.wait_ge(hid_filled[3], n + 2)
            if not isinstance(n, int):
                dve.wait_ge(ht_filled[3], n)
            e = nc.vector.value_load(TAB[0:1, 0, bass.ds(n, 1)], min_val=0, max_val=NE - 1)
            V.tensor_tensor(HR[:, a, :], PS[:, 2 + a, 0:FH], BH[:, bass.ds(e, 1), :].rearrange("p a b -> p (a b)"),
                            ALU.add).then_inc(hid_summed[3], 1)

        V.drain().then_inc(hid_summed[3], 1)
        hidden_bias(0, 0)
        with nc.vector.Fori(0, turns3) as i:
            for a in range(2):
                hidden_bias(i * 2 + a + 1, 1 - a)
        gather_sum(3)
        V.drain().then_inc(done, 1)

    block_ctx.__exit__(None, None, None)


def kernel(x, src, dst, L0_gnn_W, L0_gnn_attn_l, L0_gnn_attn_r, L0_gnn_W_res, L0_mix_w_qkv, L0_mix_w_proj,
           L0_mix_b_proj, L0_ffn_router_w, L0_ffn_router_b, L0_ffn_expert_w, L0_ffn_expert_b, L1_gnn_W1, L1_gnn_b1,
           L1_gnn_W2, L1_gnn_b2, L1_mix_w_qkv, L1_mix_w_proj, L1_mix_b_proj, L1_ffn_Wg, L1_ffn_bg, L1_ffn_W1,
           L1_ffn_b1, L1_ffn_W2, L1_ffn_b2):
    import numpy as _np
    import concourse.bacc as _bacc
    from concourse.bass_utils import run_bass_kernel_spmd as _run

    g = _np.asarray
    attn = _np.concatenate([g(L0_gnn_attn_l)[0], g(L0_gnn_attn_r)[0]], axis=0).T
    given = [("x", g(x)), ("src", g(src)), ("dst", g(dst)), ("gW", g(L0_gnn_W)), ("gWT", g(L0_gnn_W).T),
             ("gWresT", g(L0_gnn_W_res).T), ("attnT", attn), ("w0", g(L0_mix_w_qkv)), ("wp0", g(L0_mix_w_proj)),
             ("bp0", g(L0_mix_b_proj)), ("rwT", g(L0_ffn_router_w).T), ("rb", g(L0_ffn_router_b)),
             ("ewT", g(L0_ffn_expert_w).transpose(0, 2, 1)), ("eb", g(L0_ffn_expert_b)), ("W1", g(L1_gnn_W1)),
             ("b1c", g(L1_gnn_b1).reshape(KC, P).T), ("W2", g(L1_gnn_W2)), ("b2", g(L1_gnn_b2)), ("w1", g(L1_mix_w_qkv)),
             ("wp1", g(L1_mix_w_proj)), ("bp1", g(L1_mix_b_proj)), ("fgT", g(L1_ffn_Wg).T), ("fbg", g(L1_ffn_bg)),
             ("fW1", g(L1_ffn_W1)), ("fb1", g(L1_ffn_b1)), ("fW2", g(L1_ffn_W2)), ("fb2", g(L1_ffn_b2))]
    nc = _bacc.Bacc("TRN2", target_bir_lowering=False, num_devices=1)
    arrays, args = {}, {}
    for name, a in given:
        a = _np.ascontiguousarray(a)
        arrays[f"in_{name}"] = a
        args[name] = nc.dram_tensor(f"in_{name}", a.shape, mybir.dt.from_np(a.dtype), kind="ExternalInput").ap()
    out = nc.dram_tensor("out_x", (N, C), F32, kind="ExternalOutput").ap()
    xn_d = nc.dram_tensor("xn_rows", (N, C), F32).ap()
    y_d = nc.dram_tensor("expert_rows", (ET_MAX * P, C), F32).ap()
    graph_transformer(nc, xn_d, y_d, out=out, **args)
    r = _run(nc, [arrays], core_ids=[0])
    return r.results[0]["out_x"]
```
